# Optimizing a Trainium2 kernel written in Bass

```python
import numpy as np
import jax
import jax.numpy as jnp

def _softmax(x, axis=-1):
    return jax.nn.softmax(x, axis=axis)

def _gelu(x):
    return jax.nn.gelu(x, approximate=True)

def _silu(x):
    return jax.nn.silu(x)

def _sigmoid(x):
    return jax.nn.sigmoid(x)

def _layernorm(x, axis=-1, eps=1e-05):
    m = jnp.mean(x, axis=axis, keepdims=True)
    v = jnp.var(x, axis=axis, keepdims=True)
    return (x - m) / jnp.sqrt(v + eps)

def _scatter_add(tgt, idx, src, axis=0):
    return tgt.at[idx].add(src)

def _segment_sum(src, seg, n):
    return jax.ops.segment_sum(src, seg, n)
kernel_name = 'mk_conv_seq_d2_conv_nhwc256_r4_544317'

def setup_inputs(seed: int=0):
    np.random.seed(seed)
    _w = jnp.asarray

    def _rec_inputs():
        import jax
        import jax.numpy as jnp
        _gk = jax.random.key(seed)
        x = -0.0002928 + 1 * jax.random.normal(jax.random.fold_in(_gk, 1), (4, 16, 16, 64), jnp.float32)
        return x
    x = _rec_inputs()

    def _L0_conv_setup():
        import jax, jax.numpy as jnp
        import numpy as np
        N_GROUPS = 8
        N_HEADS = 4
        EPS = 1e-05

        def _group_norm(x, scale, bias):
            B, H, W, C = x.shape
            g = N_GROUPS
            xg = x.reshape(B, H, W, g, C // g)
            mean = xg.mean(axis=(1, 2, 4), keepdims=True)
            var = xg.var(axis=(1, 2, 4), keepdims=True)
            xn = ((xg - mean) * jax.lax.rsqrt(var + EPS)).reshape(B, H, W, C)
            return xn * scale + bias
        key = jax.random.key(seed)
        ks = jax.random.split(key, 4)
        B, H, W, C = (4, 16, 16, 64)
        x = jax.random.normal(ks[0], (B, H, W, C), dtype=jnp.float32)
        gn_scale = jnp.ones((C,), dtype=jnp.float32)
        gn_bias = jnp.zeros((C,), dtype=jnp.float32)
        w_qkv = jax.random.normal(ks[1], (C, 3 * C), dtype=jnp.float32) * C ** (-0.5)
        w_out = jax.random.normal(ks[2], (C, C), dtype=jnp.float32) * C ** (-0.5)
        b_out = jnp.zeros((C,), dtype=jnp.float32)
        return {'x': x, 'gn_scale': gn_scale, 'gn_bias': gn_bias, 'w_qkv': w_qkv, 'w_out': w_out, 'b_out': b_out}
    _L0_conv_all = _L0_conv_setup()
    _L0_conv_in = {k: v for k, v in _L0_conv_all.items() if k in ('gn_scale', 'gn_bias', 'w_qkv', 'w_out', 'b_out')}
    del _L0_conv_all

    def _L1_conv_setup():
        import jax, jax.numpy as jnp
        import numpy as np
        UNITS = 64
        GROUPS = 8
        EPS = 0.001

        def group_norm(x, gamma, beta, groups=GROUPS, eps=EPS):
            B, H, W, C = x.shape
            xg = x.reshape(B, H, W, groups, C // groups)
            mean = xg.mean(axis=(1, 2, 4), keepdims=True)
            var = xg.var(axis=(1, 2, 4), keepdims=True)
            xn = (xg - mean) * jax.lax.rsqrt(var + eps)
            xn = xn.reshape(B, H, W, C)
            return xn * gamma + beta
        key = jax.random.key(seed)
        ks = jax.random.split(key, 10)
        B, H, W, C = (4, 16, 16, UNITS)
        s = 1.0 / np.sqrt(C)
        x = jax.random.normal(ks[0], (B, H, W, C), dtype=jnp.float32)
        return {'x': x, 'gamma': jnp.ones((C,), jnp.float32), 'beta': jnp.zeros((C,), jnp.float32), 'Wq': jax.random.uniform(ks[1], (C, C), jnp.float32, -s, s), 'bq': jnp.zeros((C,), jnp.float32), 'Wk': jax.random.uniform(ks[2], (C, C), jnp.float32, -s, s), 'bk': jnp.zeros((C,), jnp.float32), 'Wv': jax.random.uniform(ks[3], (C, C), jnp.float32, -s, s), 'bv': jnp.zeros((C,), jnp.float32), 'Wp': jax.random.uniform(ks[4], (C, C), jnp.float32, -1e-05, 1e-05), 'bp': jnp.zeros((C,), jnp.float32)}
    _L1_conv_all = _L1_conv_setup()
    _L1_conv_in = {k: v for k, v in _L1_conv_all.items() if k in ('gamma', 'beta', 'Wq', 'bq', 'Wk', 'bk', 'Wv', 'bv', 'Wp', 'bp')}
    del _L1_conv_all
    return {'x': x, 'L0_conv_gn_scale': _L0_conv_in['gn_scale'], 'L0_conv_gn_bias': _L0_conv_in['gn_bias'], 'L0_conv_w_qkv': _L0_conv_in['w_qkv'], 'L0_conv_w_out': _L0_conv_in['w_out'], 'L0_conv_b_out': _L0_conv_in['b_out'], 'L1_conv_gamma': _L1_conv_in['gamma'], 'L1_conv_beta': _L1_conv_in['beta'], 'L1_conv_Wq': _L1_conv_in['Wq'], 'L1_conv_bq': _L1_conv_in['bq'], 'L1_conv_Wk': _L1_conv_in['Wk'], 'L1_conv_bk': _L1_conv_in['bk'], 'L1_conv_Wv': _L1_conv_in['Wv'], 'L1_conv_bv': _L1_conv_in['bv'], 'L1_conv_Wp': _L1_conv_in['Wp'], 'L1_conv_bp': _L1_conv_in['bp']}

def reference(x, L0_conv_gn_scale, L0_conv_gn_bias, L0_conv_w_qkv, L0_conv_w_out, L0_conv_b_out, L1_conv_gamma, L1_conv_beta, L1_conv_Wq, L1_conv_bq, L1_conv_Wk, L1_conv_bk, L1_conv_Wv, L1_conv_bv, L1_conv_Wp, L1_conv_bp):
    import jax
    import jax.numpy as jnp

    def _L0_conv_ref(x, gn_scale, gn_bias, w_qkv, w_out, b_out):
        import jax, jax.numpy as jnp
        import numpy as np
        N_GROUPS = 8
        N_HEADS = 4
        EPS = 1e-05

        def _group_norm(x, scale, bias):
            B, H, W, C = x.shape
            g = N_GROUPS
            xg = x.reshape(B, H, W, g, C // g)
            mean = xg.mean(axis=(1, 2, 4), keepdims=True)
            var = xg.var(axis=(1, 2, 4), keepdims=True)
            xn = ((xg - mean) * jax.lax.rsqrt(var + EPS)).reshape(B, H, W, C)
            return xn * scale + bias
        B, H, W, C = x.shape
        hd = C // N_HEADS
        scale = C ** (-0.5)
        xn = _group_norm(x, gn_scale, gn_bias)
        qkv = jnp.einsum('bhwc,cd->bhwd', xn, w_qkv)
        qkv = qkv.reshape(B, H * W, N_HEADS, 3 * hd)
        q, k, v = jnp.split(qkv, 3, axis=-1)
        atten = jnp.einsum('bihd,bjhd->bijh', q, k) * scale
        atten = jax.nn.softmax(atten, axis=2)
        res = jnp.einsum('bijh,bjhd->bihd', atten, v)
        res = res.reshape(B, H, W, C)
        res = jnp.einsum('bhwc,cd->bhwd', res, w_out) + b_out
        return res + xn

    def _L1_conv_ref(x, gamma, beta, Wq, bq, Wk, bk, Wv, bv, Wp, bp):
        import jax, jax.numpy as jnp
        import numpy as np
        UNITS = 64
        GROUPS = 8
        EPS = 0.001

        def group_norm(x, gamma, beta, groups=GROUPS, eps=EPS):
            B, H, W, C = x.shape
            xg = x.reshape(B, H, W, groups, C // groups)
            mean = xg.mean(axis=(1, 2, 4), keepdims=True)
            var = xg.var(axis=(1, 2, 4), keepdims=True)
            xn = (xg - mean) * jax.lax.rsqrt(var + eps)
            xn = xn.reshape(B, H, W, C)
            return xn * gamma + beta
        B, H, W, C = x.shape
        scale = jnp.float32(C) ** (-0.5)
        xn = group_norm(x, gamma, beta)
        n = H * W
        xf = xn.reshape(B, n, C)
        q = xf @ Wq + bq
        k = xf @ Wk + bk
        v = xf @ Wv + bv
        attn = jnp.einsum('bnc,bmc->bnm', q, k) * scale
        attn = jax.nn.softmax(attn, axis=-1)
        out = jnp.einsum('bnm,bmc->bnc', attn, v)
        out = out @ Wp + bp
        return xn + out.reshape(B, H, W, C)

    def _gn(v, G=32, eps=1e-05):
        B_, H_, W_, C_ = v.shape
        g = v.reshape(B_, H_, W_, G, C_ // G)
        m = jnp.mean(g, axis=(1, 2, 4), keepdims=True)
        s = jnp.var(g, axis=(1, 2, 4), keepdims=True)
        return ((g - m) / jnp.sqrt(s + eps)).reshape(v.shape)

    def _ln_c(v, eps=1e-06):
        m = jnp.mean(v, axis=-1, keepdims=True)
        s = jnp.var(v, axis=-1, keepdims=True)
        return (v - m) / jnp.sqrt(s + eps)

    def _ln_t(v, eps=1e-05):
        m = jnp.mean(v, axis=-1, keepdims=True)
        s = jnp.var(v, axis=-1, keepdims=True)
        return (v - m) / jnp.sqrt(s + eps)

    def _to_tokens(v):
        B_, H_, W_, C_ = v.shape
        return v.reshape(B_, H_ * W_, C_)

    def _from_tokens(t, like):
        return t.reshape(like.shape)
    x = _L0_conv_ref(x, L0_conv_gn_scale, L0_conv_gn_bias, L0_conv_w_qkv, L0_conv_w_out, L0_conv_b_out)
    x = _L1_conv_ref(x, L1_conv_gamma, L1_conv_beta, L1_conv_Wq, L1_conv_bq, L1_conv_Wk, L1_conv_bk, L1_conv_Wv, L1_conv_bv, L1_conv_Wp, L1_conv_bp)
    return x

_drawn_inputs = setup_inputs


def setup_inputs(seed=0):
    import zlib

    import numpy as np

    out = dict(_drawn_inputs(seed))
    spreads = {'L0_conv_gn_scale': (1.0, 0.2),
     'L0_conv_gn_bias': (0.0, 0.1),
     'L0_conv_b_out': (0.0, 0.1),
     'L1_conv_gamma': (1.0, 0.2),
     'L1_conv_beta': (0.0, 0.1),
     'L1_conv_bq': (0.0, 2.0),
     'L1_conv_bk': (0.0, 0.8),
     'L1_conv_bv': (0.0, 2.0),
     'L1_conv_bp': (0.0, 0.1)}
    factors = {'L1_conv_Wq': 64.0, 'L1_conv_Wk': 64.0, 'L1_conv_Wv': 64.0, 'L1_conv_Wp': 64.0}
    for name, (base, spread) in spreads.items():
        noise = np.random.default_rng([zlib.crc32(name.encode()), seed]).standard_normal(out[name].shape)
        drawn = base * np.exp(spread * noise) if base else spread * noise
        out[name] = jnp.asarray(drawn.astype(out[name].dtype))
    for name, factor in factors.items():
        out[name] = (out[name] * factor).astype(out[name].dtype)
    return out
```

```python
from contextlib import ExitStack

import numpy as np

import concourse.bass as bass
from concourse import mybir

F32 = mybir.dt.float32
F32R = mybir.dt.float32r
ALU = mybir.AluOpType
ACT = mybir.ActivationFunctionType
AX_X = mybir.AxisListType.X

B, N, C = 4, 256, 64
HALF = 128
HEADS = 4
HD = C // HEADS
PAIRS = HEADS // 2
GROUPS = 8
SCALE = float(C) ** -0.5
EPS0, EPS1 = 1e-5, 1e-3
HW = 32
RING = 4

_cols = {}
_width = [0]


def _place(name, width):
    _cols[name] = (_width[0], _width[0] + width)
    _width[0] += width


for _n, _w in (("ident", 128), ("group", C), ("vec", 16)):
    _place(_n, _w)
END_A = _width[0]
for _n, _w in (("qk", 4 * 128), ("v0", C), ("out0", C)):
    _place(_n, _w)
END_B = _width[0]
for _n, _w in (("q1", 128), ("k1", 128), ("eye2", C), ("sel", 2 * 128), ("ones", 128),
               ("v1t", 128), ("p1", C), ("bp", C)):
    _place(_n, _w)
WIDTH = _width[0]
(V_SCALE0, V_BIAS0, V_BOUT, V_SCALE1, V_BIAS1, V_BQ, V_BK, V_BV, V_QMASK, V_KMASK) = range(10)


def tokens(dram):
    return dram.rearrange("b h w c -> b (h w) c").rearrange("b (p t) c -> p b (t c)", t=2)


def build(nc, x, params, out):
    with ExitStack() as ctx:
        def sb(name, shape, dt=F32):
            return ctx.enter_context(nc.sbuf_tensor(name, shape, dt))

        def sem(name):
            return ctx.enter_context(nc.semaphore(name))

        par = sb("par", [128, WIDTH])

        def P(name):
            a, z = _cols[name]
            return par[:, a:z]

        def V(i, rows=C):
            a = _cols["vec"][0] + i
            return par[0:rows, a:a + 1]

        xin = sb("xin", [128, B, HALF])
        wqk_h, wqk_l = sb("wqk_h", [128, 4, 128], F32R), sb("wqk_l", [128, 4, 128], F32R)
        wv0_h, wv0_l = sb("wv0_h", [128, C], F32R), sb("wv0_l", [128, C], F32R)
        wq1_h, wq1_l = sb("wq1_h", [128, 128], F32R), sb("wq1_l", [128, 128], F32R)
        wk1_h, wk1_l = sb("wk1_h", [128, 128], F32R), sb("wk1_l", [128, 128], F32R)
        wvn_h = sb("wvn_h", [128, 2, C], F32R)
        wvp_l = sb("wvp_l", [128, C], F32R)
        sel = sb("sel", [128, PAIRS, 128], F32R)
        ones = sb("ones", [128, 128], F32R)
        row = sb("row", [1, C])
        ones_row = sb("ones_row", [1, 128])
        half = sb("half", [C, B])
        bn = sb("bn", [C, B, 6])
        mv = sb("mv", [C, B, 2])
        dev = sb("dev", [C, B])
        spread = sb("spread", [C, B])
        nmean = sb("nmean", [C, B])
        var = sb("var", [C, B])
        rstd = sb("rstd", [C, B])
        sc = sb("sc", [C, B])
        tb = sb("tb", [C, B])
        bn1, mv1 = sb("bn1", [C, 6]), sb("mv1", [C, 2])
        small1 = sb("small1", [C, 8])
        xn0 = sb("xn0", [C, B, N])
        xs0 = sb("xs0", [128, B, N], F32R)
        qs = sb("qs", [128, 2, PAIRS, N], F32R)
        ks = sb("ks", [128, 2, PAIRS, N], F32R)
        v0 = sb("v0", [128, B, 2, HEADS, HW])
        nmax = sb("nmax", [128, HEADS, 2])
        mcol = sb("mcol", [128, 2, 128], F32R)
        mrow = sb("mrow", [128, 2, N], F32R)
        pt = sb("pt", [128, 2, HEADS, 2, N])
        ot = sb("ot", [128, N])
        rden = sb("rden", [128, 8])
        rn = sb("rn", [128, 8, 32])
        rt = sb("rt", [128, N])
        y1 = sb("y1", [C, N])
        xn1 = sb("xn1", [C, N])
        xs1 = sb("xs1", [128, N], F32R)
        qs1 = sb("qs1", [128, N], F32R)
        kh1, kl1 = sb("kh1", [128, N], F32R), sb("kl1", [128, N], F32R)
        vn = sb("vn", [128, 2, 2, C + 1])
        nmax1 = sb("nmax1", [128, 2])
        mcol1 = sb("mcol1", [128, 2, 2], F32R)
        mrow1 = sb("mrow1", [2, N], F32R)
        pt1 = sb("pt1", [128, 2, N])
        rden1 = sb("rden1", [128, 2])
        res = sb("res", [128, B, 2, C])

        ring = [ctx.enter_context(nc.psum_tensor(f"ring{i}", [128, 2, N], F32)) for i in range(RING)]
        bank_q = ctx.enter_context(nc.psum_tensor("bank_q", [128, 512], F32))
        bank_k = ctx.enter_context(nc.psum_tensor("bank_k", [128, 512], F32))
        bank_m = ctx.enter_context(nc.psum_tensor("bank_m", [128, 512], F32))
        bank_o = ctx.enter_context(nc.psum_tensor("bank_o", [128, 512], F32))

        x_in = [sem(f"x_in{i}") for i in range(2)]
        a_in, b_in, c_in = sem("a_in"), sem("b_in"), sem("c_in")
        out_sent = sem("out_sent")
        xt_ready = sem("xt_ready")
        hop_ready = sem("hop_ready")
        spread_ready = sem("spread_ready")
        rstd_ready = sem("rstd_ready")
        xn_ready = sem("xn_ready")
        xhi_ready = sem("xhi_ready")
        xs_ready = sem("xs_ready")
        w0_hi, w0_lo = sem("w0_hi"), sem("w0_lo")
        w1_hi, w1_lo = sem("w1_hi"), sem("w1_lo")
        const_ready = sem("const_ready")
        q_made, k_made, v_made = sem("q_made"), sem("k_made"), sem("v_made")
        q_hi, k_hi = sem("q_hi"), sem("k_hi")
        q_ready, k_ready, v_ready = sem("q_ready"), sem("k_ready"), sem("v_ready")
        s_made = sem("s_made")
        s_max = sem("s_max")
        mcol_ready, mrow_made = sem("mcol_ready"), sem("mrow_made")
        t_made = sem("t_made")
        exp_done = sem("exp_done")
        pv_made = sem("pv_made")
        rt_ready = sem("rt_ready")
        y_made = sem("y_made")
        o_read = sem("o_read")
        m_read = sem("m_read")
        xn1_ready, xhi1_ready, xs1_ready = sem("xn1_ready"), sem("xhi1_ready"), sem("xs1_ready")
        q1_made, k1_made = sem("q1_made"), sem("k1_made")
        q1_hi, k1_hi, vn_ready = sem("q1_hi"), sem("k1_hi"), sem("vn_ready")
        q1_ready, k1_ready = sem("q1_ready"), sem("k1_ready")
        s1_made, s1_max = sem("s1_made"), sem("s1_max")
        mcol1_ready, mrow1_made = sem("mcol1_ready"), sem("mrow1_made")
        t1_made, exp1_done, pv1_made = sem("t1_made"), sem("exp1_done"), sem("pv1_made")
        wvp_made, wvp_hi, wvp_ready = sem("wvp_made"), sem("wvp_hi"), sem("wvp_ready")
        dve_step = sem("dve_step")

        ROUNDS = range(-2, B + 1)
        ring_order = [("X", b) for b in range(B)]
        q_order, k_order, m_order, o_order = [("WV", 0)], [], [("H0", 0), ("H0", 1)], []
        for r in ROUNDS:
            b, n, m, l = r, r + 1, r + 2, r - 1
            for h in range(HEADS):
                ring_order += [("S", n, h)] * (0 <= n < B) + [("T", b, h)] * (0 <= b < B)
            ring_order += [("S1", l), ("T1", l)] * (0 <= l < B)
            q_order += [("QV1", l)] * (0 <= l < B) + [("Q", m), ("V", m)] * (m < B)
            k_order += [("K1", l)] * (0 <= l < B) + [("K", m)] * (m < B)
            m_order += ([("H1", l, 0), ("H1", l, 1)] * (0 <= l < B) + [("MR", n)] * (0 <= n < B)
                        + [("MR1", l)] * (0 <= l < B))
            o_order += [("PV", b), ("Y", b)] * (0 <= b < B) + [("PV1", l)] * (0 <= l < B)
        read_by = {"X": xn_ready, "S": s_max, "T": exp_done, "S1": s1_max, "T1": exp1_done,
                   "WV": wvp_ready, "Q": q_ready, "V": v_ready, "QV1": q1_ready, "K": k_ready, "K1": k1_ready}

        def m_reads(*key):
            return m_order.index(key) + 1

        def o_reads(*key):
            return o_order.index(key) + 1

        def bank(*key):
            return ring[ring_order.index(key) % RING]

        def wait_bank(pe, order, *key):
            i = order.index(key) - (RING if order is ring_order else 1)
            if i < 0:
                return
            if order is m_order:
                pe.wait_ge(m_read, i + 1)
            elif order is o_order:
                pe.wait_ge(o_read, i + 1)
            else:
                kind, b, *h = order[i]
                pe.wait_ge(read_by[kind], b * HEADS + h[0] + 1 if h else b + 1)

        block = ctx.enter_context(nc.Block())

        @block.sync
        def _(sp):
            for i in range(2):
                sp.dma_start(xin[:, 2 * i:2 * i + 2, :], tokens(x)[:, 2 * i:2 * i + 2, :]).then_inc(x_in[i], 16)
            sp.dma_start(par[:, END_B:WIDTH], params[:, END_B:WIDTH]).then_inc(c_in, 16)
            for b in range(B):
                sp.wait_ge(o_read, o_reads("PV1", b))
                sp.dma_start(tokens(out)[:, b, :], res[:, b, :, :].rearrange("p t c -> p (t c)")).then_inc(out_sent, 16)
            sp.wait_ge(out_sent, 16 * B)

        @block.gpsimd
        def _(pool):
            nc.gpsimd.memset(half[:], -0.5).then_inc(const_ready, 1)
            nc.gpsimd.memset(rn[:], 0.0).then_inc(const_ready, 1)
            nc.gpsimd.memset(mcol[:].bitcast(F32), 0.0).then_inc(const_ready, 1)
            nc.gpsimd.memset(v0[:], 1.0).then_inc(const_ready, 1)
            nc.gpsimd.memset(vn[:], 1.0).then_inc(const_ready, 1)
            nc.gpsimd.memset(ones_row[:], 1.0).then_inc(const_ready, 1)
            pool.wait_ge(const_ready, 1)
            pool.wait_ge(m_read, m_reads("H0", 1))
            nc.gpsimd.tensor_tensor(rstd[:], var[:], half[:], ALU.pow).then_inc(rstd_ready, 1)
            for b in range(B):
                pool.wait_ge(m_read, m_reads("H1", b, 1))
                nc.gpsimd.tensor_tensor(small1[:, 3:4], small1[:, 2:3], half[:, 0:1], ALU.pow).then_inc(rstd_ready, 1)

        @block.scalar
        def _(act):
            act.dma_start(par[:, 0:END_A], params[:, 0:END_A]).then_inc(a_in, 16)
            act.dma_start(par[:, END_A:END_B], params[:, END_A:END_B]).then_inc(b_in, 16)

            act.wait_ge(b_in, 16)
            nc.scalar.copy(wqk_h[:], P("qk").rearrange("p (m c) -> p m c", m=4)).then_inc(w0_hi, 1)
            nc.scalar.copy(wv0_h[:], P("v0")).then_inc(w0_hi, 1)

            def x_hi(b):
                act.wait_ge(xn_ready, b + 1)
                nc.scalar.copy(xs0[0:C, b, :], xn0[:, b, :]).then_inc(xhi_ready, 1)

            def qk_hi(b):
                if b >= 2:
                    act.wait_ge(t_made, HEADS * (b - 1))
                act.wait_ge(q_made, b + 1)
                nc.scalar.copy(qs[:, b % 2, :, :], bank_q[:, :].rearrange("p (m n) -> p m n", m=PAIRS)).then_inc(q_hi, 1)
                act.wait_ge(k_made, b + 1)
                nc.scalar.copy(ks[:, b % 2, :, :], bank_k[:, :].rearrange("p (m n) -> p m n", m=PAIRS)).then_inc(k_hi, 1)

            def v_copy(b):
                act.wait_ge(const_ready, 4)
                act.wait_ge(v_made, b + 1)
                nc.scalar.copy(v0[:, b, :, :, 0:HD],
                               bank_q[:, 0:2 * C].rearrange("p (t h d) -> p t h d", t=2, h=HEADS)).then_inc(v_ready, 1)

            def exp(b, h):
                act.wait_ge(t_made, HEADS * b + h + 1)
                if b >= 2:
                    act.wait_ge(pv_made, b - 1)
                nc.scalar.activation(pt[:, b % 2, h, :, :], bank("T", b, h)[:, :, :], ACT.Exp,
                                     scale=SCALE).then_inc(exp_done, 1)

            def x_hi1(b):
                act.wait_ge(xn1_ready, b + 1)
                if b >= 1:
                    act.wait_ge(k1_made, b)
                nc.scalar.copy(xs1[0:C, :], xn1[:, :]).then_inc(xhi1_ready, 1)

            def qkv_hi1(b):
                act.wait_ge(q1_made, b + 1)
                if b >= 1:
                    act.wait_ge(pv1_made, b)
                nc.scalar.activation(qs1[0:C, :], bank_q[0:C, 0:N], ACT.Identity, bias=V(V_BQ)).then_inc(q1_hi, 1)
                act.wait_ge(const_ready, 5)
                if b >= 1:
                    act.wait_ge(o_read, o_reads("PV1", b - 1))
                nc.scalar.copy(vn[:, :, :, 0:C], bank_q[:, N:2 * N].rearrange("p (t g c) -> p t g c", t=2, g=2)).then_inc(vn_ready, 1)
                act.wait_ge(k1_made, b + 1)
                nc.scalar.activation(kh1[:, :], bank_k[:, 0:N], ACT.Identity, bias=V(V_BK, 128)).then_inc(k1_hi, 1)

            def exp1(b):
                act.wait_ge(t1_made, b + 1)
                if b >= 1:
                    act.wait_ge(pv1_made, b)
                nc.scalar.activation(pt1[:, :, :], bank("T1", b)[:, :, :], ACT.Exp, scale=SCALE).then_inc(exp1_done, 1)

            def weights1_hi():
                act.wait_ge(c_in, 16)
                nc.scalar.copy(wq1_h[:], P("q1")).then_inc(w1_hi, 1)
                nc.scalar.copy(wk1_h[:], P("k1")).then_inc(w1_hi, 1)
                nc.scalar.copy(wvn_h[:, 1, :], P("eye2")).then_inc(w1_hi, 1)
                nc.scalar.copy(sel[:], P("sel").rearrange("p (m c) -> p m c", m=PAIRS)).then_inc(w1_hi, 1)
                nc.scalar.copy(ones[:], P("ones")).then_inc(w1_hi, 1)
                act.wait_ge(wvp_made, 1)
                nc.scalar.copy(wvn_h[:, 0, :], bank_q[:, 256:256 + C]).then_inc(wvp_hi, 1)

            x_hi(0)
            weights1_hi()
            for b in range(1, B):
                x_hi(b)
            for r in ROUNDS:
                b, n, m, l = r, r + 1, r + 2, r - 1
                if 0 <= l < B:
                    x_hi1(l)
                if 0 <= b < B:
                    exp(b, 0)
                    exp(b, 1)
                if 0 <= l < B:
                    qkv_hi1(l)
                if 0 <= b < B:
                    exp(b, 2)
                    exp(b, 3)
                if m < B:
                    qk_hi(m)
                    v_copy(m)
                if 0 <= l < B:
                    exp1(l)

        @block.vector
        def _(dve):
            steps = [0]

            def then(ins):
                ins.then_inc(dve_step, 1)
                steps[0] += 1
                dve.wait_ge(dve_step, steps[0])

            for b in range(B):
                dve.wait_ge(xt_ready, b + 1)
                then(nc.vector.bn_stats(bn[:, b, :], bank("X", b)[0:C, 0, :]))
                ins = nc.vector.bn_aggr(mv[:, b, :], bn[:, b, :])
                if b < B - 1:
                    then(ins)
            ins.then_inc(spread_ready, 1)
            dve.wait_ge(spread_ready, 1)
            dve.wait_ge(hop_ready, 1)
            nc.vector.tensor_tensor(dev[:], mv[:, :, 0], bank_m[0:C, 0:B], ALU.subtract).then_inc(m_read, 1)
            dve.wait_ge(m_read, 1)
            then(nc.vector.tensor_tensor(spread[:], dev[:], dev[:], ALU.mult))
            nc.vector.tensor_tensor(spread[:], spread[:], mv[:, :, 1], ALU.add).then_inc(spread_ready, 1)
            then(nc.vector.tensor_tensor(nmean[:], dev[:], mv[:, :, 0], ALU.subtract))
            dve.wait_ge(hop_ready, 2)
            nc.vector.tensor_scalar(var[:], bank_m[0:C, 0:B], EPS0, None, ALU.add).then_inc(m_read, 1)
            dve.wait_ge(a_in, 16)
            dve.wait_ge(rstd_ready, 1)
            then(nc.vector.tensor_scalar(sc[:], rstd[:], V(V_SCALE0), None, ALU.mult))
            then(nc.vector.tensor_tensor(tb[:], nmean[:], sc[:], ALU.mult))
            then(nc.vector.tensor_scalar(tb[:], tb[:], V(V_BIAS0), None, ALU.add))

            def x_norm(b):
                nc.vector.tensor_scalar(xn0[:, b, :], bank("X", b)[0:C, 0, :],
                                        sc[:, b:b + 1], tb[:, b:b + 1], ALU.mult, ALU.add).then_inc(xn_ready, 1)

            def x_lo(b):
                dve.wait_ge(xhi_ready, b + 1)
                nc.vector.tensor_tensor(xs0[C:128, b, :], xn0[:, b, :], xs0[0:C, b, :].bitcast(F32),
                                        ALU.subtract).then_inc(xs_ready, 1)

            def weights0_lo():
                dve.wait_ge(w0_hi, 2)
                nc.vector.tensor_tensor(wqk_l[:], P("qk").rearrange("p (m c) -> p m c", m=4),
                                        wqk_h[:].bitcast(F32), ALU.subtract).then_inc(w0_lo, 1)
                nc.vector.tensor_tensor(wv0_l[:], P("v0"), wv0_h[:].bitcast(F32), ALU.subtract).then_inc(w0_lo, 1)

            def weights1_lo():
                dve.wait_ge(w1_hi, 5)
                nc.vector.tensor_tensor(wq1_l[:], P("q1"), wq1_h[:].bitcast(F32), ALU.subtract).then_inc(w1_lo, 1)
                nc.vector.tensor_tensor(wk1_l[:], P("k1"), wk1_h[:].bitcast(F32), ALU.subtract).then_inc(w1_lo, 1)
                dve.wait_ge(wvp_hi, 1)
                nc.vector.tensor_tensor(wvp_l[:], bank_q[:, 256:256 + C], wvn_h[:, 0, :].bitcast(F32),
                                        ALU.subtract)
                nc.vector.tensor_tensor(row[:], bank_q[0:1, 384:384 + C], P("bp")[0:1, :], ALU.add).then_inc(wvp_ready, 1)

            def qk_lo(b):
                for hi, lo, src, dst, mask in ((q_hi, q_ready, bank_q, qs, V_QMASK), (k_hi, k_ready, bank_k, ks, V_KMASK)):
                    dve.wait_ge(hi, b + 1)
                    nc.vector.scalar_tensor_tensor(dst[:, b % 2, :, :], dst[:, b % 2, :, :].bitcast(F32), V(mask, 128),
                                                   src[:, :].rearrange("p (m n) -> p m n", m=PAIRS),
                                                   ALU.mult, ALU.add).then_inc(lo, 1)

            def smax(b, h):
                dve.wait_ge(s_made, HEADS * b + h + 1)
                if h == 0 and b >= 1:
                    dve.wait_ge(mcol_ready, 2 * b)
                nc.vector.tensor_reduce(nmax[:, h, :], bank("S", b, h)[:, :, :], AX_X, ALU.max, negate=True).then_inc(s_max, 1)

            def max_cols(b):
                dve.wait_ge(s_max, HEADS * (b + 1))
                dve.wait_ge(const_ready, 3)
                if b >= 1:
                    dve.wait_ge(mrow_made, b)
                src = nmax[:, :, :].rearrange("q (p s) t -> q p s t", s=2)
                dst = mcol[:, :, :].rearrange("q t (s r) -> q t s r", s=2)
                for part in range(2):
                    for s in range(2):
                        d = dst[:, :, s, part:part + 3:2].rearrange("q t p -> q p t")
                        if part == 0:
                            ins = nc.vector.tensor_copy(d, src[:, :, s, :])
                        else:
                            hi = dst[:, :, s, 0:3:2].rearrange("q t p -> q p t").bitcast(F32)
                            ins = nc.vector.tensor_tensor(d, src[:, :, s, :], hi, ALU.subtract)
                    ins.then_inc(mcol_ready, 1)
                    if part == 0:
                        dve.wait_ge(mcol_ready, 2 * b + 1)

            def max_rows(b):
                dve.wait_ge(mrow_made, b + 1)
                if b >= 2:
                    dve.wait_ge(t_made, HEADS * (b - 1))
                nc.vector.tensor_copy(mrow[:, b % 2, :], bank_m[:, 0:N]).then_inc(m_read, 1)

            def norm_out(b):
                dve.wait_ge(pv_made, b + 1)
                nc.vector.transpose(ot[:], bank_o[:, 0:N]).then_inc(o_read, 1)
                dve.wait_ge(o_read, o_reads("PV", b))
                blocks = ot[:, :].rearrange("p (k r) -> p k r", r=32)
                then(nc.vector.reciprocal(rden[:, :], blocks[:, :, HD]))
                dve.wait_ge(const_ready, 2)
                then(nc.vector.tensor_tensor(rn[:, :, 0:HD], blocks[:, :, 0:HD],
                                             rden[:, :].unsqueeze(2).broadcast_to([128, 8, HD]), ALU.mult))
                if b >= 1:
                    dve.wait_ge(y_made, b)
                nc.vector.transpose(rt[:], rn[:, :, :].rearrange("p k r -> p (k r)")).then_inc(rt_ready, 1)

            def residual(b):
                dve.wait_ge(y_made, b + 1)
                nc.vector.scalar_tensor_tensor(y1[:, :], bank_o[0:C, 0:N], V(V_BOUT), xn0[:, b, :],
                                               ALU.add, ALU.add).then_inc(o_read, 1)
                dve.wait_ge(o_read, o_reads("Y", b))

            def stats1(b):
                then(nc.vector.bn_stats(bn1[:], y1[:, :]))
                nc.vector.bn_aggr(mv1[:], bn1[:]).then_inc(spread_ready, 1)
                dve.wait_ge(spread_ready, 2 * b + 3)

            def stats1_spread(b):
                dve.wait_ge(hop_ready, 2 * b + 3)
                nc.vector.tensor_tensor(small1[:, 0:1], mv1[:, 0:1], bank_m[0:C, 0:1], ALU.subtract).then_inc(m_read, 1)
                dve.wait_ge(m_read, m_reads("H1", b, 0))
                nc.vector.scalar_tensor_tensor(small1[:, 1:2], small1[:, 0:1], small1[:, 0:1], mv1[:, 1:2],
                                               ALU.mult, ALU.add).then_inc(spread_ready, 1)
                then(nc.vector.tensor_tensor(small1[:, 6:7], small1[:, 0:1], mv1[:, 0:1], ALU.subtract))

            def stats1_var(b):
                dve.wait_ge(hop_ready, 2 * b + 4)
                nc.vector.tensor_scalar(small1[:, 2:3], bank_m[0:C, 0:1], EPS1, None, ALU.add).then_inc(m_read, 1)

            def x_norm1(b):
                dve.wait_ge(rstd_ready, b + 2)
                then(nc.vector.tensor_scalar(small1[:, 4:5], small1[:, 3:4], V(V_SCALE1), None, ALU.mult))
                then(nc.vector.scalar_tensor_tensor(small1[:, 5:6], small1[:, 6:7], small1[:, 4:5], V(V_BIAS1),
                                                    ALU.mult, ALU.add))
                if b >= 1:
                    dve.wait_ge(xs1_ready, b)
                nc.vector.tensor_scalar(xn1[:, :], y1[:, :], small1[:, 4:5], small1[:, 5:6],
                                        ALU.mult, ALU.add).then_inc(xn1_ready, 1)

            def x_lo1(b):
                dve.wait_ge(xhi1_ready, b + 1)
                nc.vector.tensor_tensor(xs1[C:128, :], xn1[:, :], xs1[0:C, :].bitcast(F32),
                                        ALU.subtract).then_inc(xs1_ready, 1)

            def qk_lo1(b):
                dve.wait_ge(vn_ready, b + 1)
                dve.wait_ge(q1_hi, b + 1)
                nc.vector.scalar_tensor_tensor(qs1[C:128, :], bank_q[0:C, 0:N], V(V_BQ), qs1[0:C, :].bitcast(F32),
                                               ALU.add, ALU.subtract).then_inc(q1_ready, 1)
                dve.wait_ge(k1_hi, b + 1)
                nc.vector.scalar_tensor_tensor(kl1[:, :], bank_k[:, 0:N], V(V_BK, 128), kh1[:, :].bitcast(F32),
                                               ALU.add, ALU.subtract).then_inc(k1_ready, 1)

            def smax1(b):
                dve.wait_ge(s1_made, b + 1)
                nc.vector.tensor_reduce(nmax1[:, :], bank("S1", b)[:, :, :], AX_X, ALU.max, negate=True).then_inc(s1_max, 1)
                dve.wait_ge(s1_max, b + 1)
                if b >= 1:
                    dve.wait_ge(mrow1_made, b)
                then(nc.vector.tensor_copy(mcol1[:, :, 0], nmax1[:, :]))
                nc.vector.tensor_tensor(mcol1[:, :, 1], nmax1[:, :], mcol1[:, :, 0].bitcast(F32),
                                        ALU.subtract).then_inc(mcol1_ready, 1)

            def max_rows1(b):
                dve.wait_ge(mrow1_made, b + 1)
                nc.vector.tensor_copy(mrow1[:, :], bank_m[0:2, 0:N]).then_inc(m_read, 1)

            def final(b):
                dve.wait_ge(pv1_made, b + 1)
                o1 = bank_o[:, 0:2 * (C + 1)].rearrange("p (t c) -> p t c", t=2)
                then(nc.vector.reciprocal(rden1[:, :], o1[:, :, C]))
                for t in range(2):
                    ins = nc.vector.scalar_tensor_tensor(res[:, b, t, :], o1[:, t, 0:C], rden1[:, t:t + 1],
                                                   vn[:, t, 1, 0:C], ALU.mult, ALU.add)
                ins.then_inc(o_read, 1)

            x_norm(0)
            weights0_lo()
            x_lo(0)
            for b in range(1, B):
                x_norm(b)
            weights1_lo()
            for b in range(1, B):
                x_lo(b)
            for r in ROUNDS:
                b, n, m, l = r, r + 1, r + 2, r - 1
                if 0 <= l < B:
                    stats1(l)
                if 0 <= n < B:
                    smax(n, 0)
                if 0 <= l < B:
                    stats1_spread(l)
                if 0 <= n < B:
                    smax(n, 1)
                if 0 <= l < B:
                    stats1_var(l)
                    x_norm1(l)
                if 0 <= n < B:
                    smax(n, 2)
                if 0 <= l < B:
                    x_lo1(l)
                if 0 <= n < B:
                    smax(n, 3)
                    max_cols(n)
                if 0 <= l < B:
                    qk_lo1(l)
                if 0 <= n < B:
                    max_rows(n)
                if m < B:
                    qk_lo(m)
                if 0 <= l < B:
                    smax1(l)
                if 0 <= b < B:
                    norm_out(b)
                if 0 <= l < B:
                    max_rows1(l)
                if 0 <= b < B:
                    residual(b)
                if 0 <= l < B:
                    final(l)

        @block.tensor
        def _(pe):
            def x_transpose(b):
                pe.wait_ge(x_in[b // 2], 16)
                for t in range(2):
                    mm = pe.transpose(bank("X", b)[0:C, 0, t * HALF:(t + 1) * HALF], xin[:, b, C * t:C * (t + 1)], P("ident"))
                mm.then_inc(xt_ready, 1)

            def qk(b):
                pe.wait_ge(w0_lo, 2)
                pe.wait_ge(xs_ready, b + 1)
                for dst, first, made, order, kind in ((bank_q, 0, q_made, q_order, "Q"), (bank_k, 2, k_made, k_order, "K")):
                    wait_bank(pe, order, kind, b)
                    for p in range(PAIRS):
                        o = dst[:, p * N:(p + 1) * N]
                        pe.matmul(o, wqk_h[:, first + p, :], xs0[:, b, :], start=True, stop=False)
                        mm = pe.matmul(o, wqk_l[:, first + p, :], xs0[:, b, :], start=False, stop=True)
                    mm.then_inc(made, 1)

            def v(b):
                wait_bank(pe, q_order, "V", b)
                for t in range(2):
                    o = bank_q[:, t * C:(t + 1) * C]
                    x_t = xs0[:, b, t * HALF:(t + 1) * HALF]
                    pe.matmul(o, x_t, wv0_h[:, :], start=True, stop=False)
                    mm = pe.matmul(o, x_t, wv0_l[:, :], start=False, stop=True)
                mm.then_inc(v_made, 1)

            def rows(h):
                return slice(64 * (h % 2), 64 * (h % 2) + 64)

            def scores(b, h):
                if h == 0:
                    pe.wait_ge(q_ready, b + 1)
                    pe.wait_ge(k_ready, b + 1)
                wait_bank(pe, ring_order, "S", b, h)
                for t in range(2):
                    mm = pe.matmul(bank("S", b, h)[:, t, :], qs[rows(h), b % 2, h // 2, t * HALF:(t + 1) * HALF],
                                   ks[rows(h), b % 2, h // 2, :], start=True, stop=True)
                mm.then_inc(s_made, 1)

            def max_rows(b):
                pe.wait_ge(mcol_ready, 2 * b + 2)
                wait_bank(pe, m_order, "MR", b)
                for t in range(2):
                    mm = pe.transpose(bank_m[:, t * HALF:(t + 1) * HALF], mcol[:, t, :].bitcast(F32), P("ident"))
                mm.then_inc(mrow_made, 1)

            def scores_t(b, h):
                if h == 0:
                    pe.wait_ge(m_read, m_reads("MR", b))
                    pe.wait_ge(w1_hi, 5)
                wait_bank(pe, ring_order, "T", b, h)
                o = bank("T", b, h)
                pe.matmul(o[:, :, :], sel[rows(h), h // 2, :],
                          mrow[rows(h), b % 2, :].unsqueeze(1).broadcast_to([64, 2, N]), start=True, stop=False)
                for t in range(2):
                    mm = pe.matmul(o[:, t, :], ks[rows(h), b % 2, h // 2, t * HALF:(t + 1) * HALF],
                                   qs[rows(h), b % 2, h // 2, :], start=False, stop=(t == 1))
                mm.then_inc(t_made, 1)

            def pv(b):
                pe.wait_ge(v_ready, b + 1)
                pe.wait_ge(exp_done, HEADS * (b + 1))
                wait_bank(pe, o_order, "PV", b)
                for t in range(2):
                    for h in range(HEADS):
                        mm = pe.matmul(bank_o[HW * h:HW * (h + 1), 0:N], v0[:, b, t, h, :], pt[:, b % 2, h, t, :],
                                       start=(t == 0), stop=(t == 1))
                mm.then_inc(pv_made, 1)

            def y(b):
                pe.wait_ge(rt_ready, b + 1)
                wait_bank(pe, o_order, "Y", b)
                pe.matmul(bank_o[0:C, 0:N], P("out0"), rt[:, :], start=True, stop=True).then_inc(y_made, 1)

            def hop(b, k):
                pe.wait_ge(spread_ready, 2 * b + 3 + k)
                wait_bank(pe, m_order, "H1", b, k)
                src = mv1[:, 0:1] if k == 0 else small1[:, 1:2]
                pe.matmul(bank_m[0:C, 0:1], P("group")[0:C, :], src, start=True, stop=True).then_inc(hop_ready, 1)

            def qkv1(b):
                pe.wait_ge(w1_lo, 2)
                pe.wait_ge(const_ready, 6)
                pe.wait_ge(wvp_ready, 1)
                pe.wait_ge(xs1_ready, b + 1)
                wait_bank(pe, q_order, "QV1", b)
                for t in range(2):
                    x_t = xs1[:, t * HALF:(t + 1) * HALF]
                    o = bank_q[:, N + t * 2 * C:N + (t + 1) * 2 * C]
                    pe.matmul(o, x_t, wvn_h[:, :, :].rearrange("p g c -> p (g c)"), start=True, stop=False)
                    pe.matmul(o[:, 0:C], x_t, wvp_l[:, :], start=False, stop=False)
                    pe.matmul(o[:, C:2 * C], ones_row[0:1, :], row[0:1, :], start=False, stop=True)
                pe.matmul(bank_q[:, 0:N], wq1_h[:, :], xs1[:, :], start=True, stop=False)
                pe.matmul(bank_q[:, 0:N], wq1_l[:, :], xs1[:, :], start=False, stop=True).then_inc(q1_made, 1)
                wait_bank(pe, k_order, "K1", b)
                pe.matmul(bank_k[:, 0:N], wk1_h[:, :], xs1[:, :], start=True, stop=False)
                pe.matmul(bank_k[:, 0:N], wk1_l[:, :], xs1[:, :], start=False, stop=True).then_inc(k1_made, 1)

            def scores1(b):
                pe.wait_ge(q1_ready, b + 1)
                pe.wait_ge(k1_ready, b + 1)
                wait_bank(pe, ring_order, "S1", b)
                for t in range(2):
                    o, q_t = bank("S1", b)[:, t, :], qs1[:, t * HALF:(t + 1) * HALF]
                    pe.matmul(o, q_t, kh1[:, :], start=True, stop=False)
                    mm = pe.matmul(o, q_t, kl1[:, :], start=False, stop=True)
                mm.then_inc(s1_made, 1)

            def max_rows1(b):
                pe.wait_ge(mcol1_ready, b + 1)
                wait_bank(pe, m_order, "MR1", b)
                for t in range(2):
                    mm = pe.transpose(bank_m[0:2, t * HALF:(t + 1) * HALF], mcol1[:, t, :].bitcast(F32), P("ident"))
                mm.then_inc(mrow1_made, 1)

            def scores1_t(b):
                pe.wait_ge(m_read, m_reads("MR1", b))
                wait_bank(pe, ring_order, "T1", b)
                o = bank("T1", b)
                pe.matmul(o[:, :, :], ones[0:2, :], mrow1[:, :].unsqueeze(1).broadcast_to([2, 2, N]),
                          start=True, stop=False)
                for t in range(2):
                    pe.matmul(o[:, t, :], kh1[:, t * HALF:(t + 1) * HALF], qs1[:, :], start=False, stop=False)
                    mm = pe.matmul(o[:, t, :], kl1[:, t * HALF:(t + 1) * HALF], qs1[:, :], start=False, stop=(t == 1))
                mm.then_inc(t1_made, 1)

            def pv1(b):
                pe.wait_ge(vn_ready, b + 1)
                pe.wait_ge(exp1_done, b + 1)
                wait_bank(pe, o_order, "PV1", b)
                for t in range(2):
                    o = bank_o[:, t * (C + 1):(t + 1) * (C + 1)]
                    for j in range(2):
                        mm = pe.matmul(o, pt1[:, j, t * HALF:(t + 1) * HALF], vn[:, j, 0, :],
                                       start=(j == 0), stop=(j == 1))
                mm.then_inc(pv1_made, 1)

            pe.wait_ge(a_in, 16)
            for b in range(B):
                x_transpose(b)
            for k, src in ((0, mv[:, :, 0]), (1, spread[:, :])):
                pe.wait_ge(spread_ready, k + 1)
                pe.matmul(bank_m[0:C, 0:B], P("group")[0:C, :], src, start=True, stop=True).then_inc(hop_ready, 1)
            pe.wait_ge(c_in, 16)
            pe.matmul(bank_q[:, 256:256 + C], P("v1t")[0:C, :], P("p1")[0:C, :], start=True, stop=True)
            pe.matmul(bank_q[0:1, 384:384 + C], V(V_BV), P("p1")[0:C, :], start=True, stop=True).then_inc(wvp_made, 1)
            for r in ROUNDS:
                b, n, m, l = r, r + 1, r + 2, r - 1
                if 0 <= l < B:
                    hop(l, 0)
                if 0 <= n < B:
                    scores(n, 0)
                if 0 <= b < B:
                    scores_t(b, 0)
                if 0 <= l < B:
                    hop(l, 1)
                if 0 <= n < B:
                    scores(n, 1)
                if 0 <= b < B:
                    scores_t(b, 1)
                if 0 <= n < B:
                    scores(n, 2)
                if 0 <= b < B:
                    scores_t(b, 2)
                if 0 <= n < B:
                    scores(n, 3)
                if 0 <= b < B:
                    scores_t(b, 3)
                if 0 <= l < B:
                    qkv1(l)
                if 0 <= n < B:
                    max_rows(n)
                if m < B:
                    qk(m)
                    v(m)
                if 0 <= l < B:
                    scores1(l)
                if 0 <= b < B:
                    pv(b)
                if 0 <= l < B:
                    max_rows1(l)
                    scores1_t(l)
                if 0 <= b < B:
                    y(b)
                if 0 <= l < B:
                    pv1(l)


def kernel(x, L0_conv_gn_scale, L0_conv_gn_bias, L0_conv_w_qkv, L0_conv_w_out, L0_conv_b_out,
           L1_conv_gamma, L1_conv_beta, L1_conv_Wq, L1_conv_bq, L1_conv_Wk, L1_conv_bk,
           L1_conv_Wv, L1_conv_bv, L1_conv_Wp, L1_conv_bp):
    import concourse.bacc as bacc
    from concourse.bass_utils import run_bass_kernel_spmd

    params = np.zeros((128, WIDTH), np.float32)

    def put(name, value, rows=slice(0, 128)):
        a, z = _cols[name]
        params[rows, a:z] = value

    def twice(w):
        return np.concatenate([w, w], axis=0)

    put("ident", np.eye(128))
    size = C // GROUPS
    put("group", np.kron(np.eye(GROUPS), np.full((size, size), 1.0 / size)), slice(0, C))
    for i, vec in ((V_SCALE0, L0_conv_gn_scale), (V_BIAS0, L0_conv_gn_bias), (V_BOUT, L0_conv_b_out),
                   (V_SCALE1, L1_conv_gamma), (V_BIAS1, L1_conv_beta), (V_BQ, L1_conv_bq),
                   (V_BK, L1_conv_bk), (V_BV, L1_conv_bv)):
        params[:, _cols["vec"][0] + i] = twice(np.asarray(vec))
    part = np.arange(128) % 64 // HD
    params[:, _cols["vec"][0] + V_QMASK] = np.where(part >= 2, -1.0, 0.0)
    params[:, _cols["vec"][0] + V_KMASK] = np.where(part % 2 == 1, -1.0, 0.0)
    qkv = np.asarray(L0_conv_w_qkv).reshape(C, HEADS, 3, HD)
    stacks = [np.repeat(qkv[:, 2 * p:2 * p + 2, i, None, :], 4, axis=2).reshape(C, 128)
              for i in range(2) for p in range(PAIRS)]
    put("qk", twice(np.concatenate(stacks, axis=1)))
    put("v0", twice(qkv[:, :, 2, :].reshape(C, C)))
    w_out = np.zeros((HEADS, 32, C), np.float32)
    w_out[:, 0:HD, :] = np.asarray(L0_conv_w_out).reshape(HEADS, HD, C)
    put("out0", w_out.reshape(128, C))
    for name, w in (("q1", L1_conv_Wq), ("k1", L1_conv_Wk)):
        put(name, np.tile(np.asarray(w), (2, 2)))
    put("eye2", twice(np.eye(C)))
    picks = np.zeros((2, 64, PAIRS, 128), np.float32)
    for p in range(PAIRS):
        picks[:, 2 * p:2 * p + 2, p, :] = 1.0
    put("sel", picks.reshape(128, PAIRS * 128))
    put("ones", 1.0)
    put("v1t", np.tile(np.asarray(L1_conv_Wv).T, (2, 2)))
    put("p1", twice(np.asarray(L1_conv_Wp)))
    put("bp", np.asarray(L1_conv_bp)[None, :], slice(0, 1))

    arrays = {"x_dram": np.ascontiguousarray(x), "params_dram": params}
    nc = bacc.Bacc("TRN2", target_bir_lowering=False, num_devices=1)
    ins = [nc.dram_tensor(n, a.shape, mybir.dt.from_np(a.dtype), kind="ExternalInput").ap() for n, a in arrays.items()]
    out = nc.dram_tensor("out_0_dram", (B, 16, 16, C), F32, kind="ExternalOutput").ap()
    build(nc, ins[0], ins[1], out)
    return run_bass_kernel_spmd(nc, [arrays], core_ids=[0]).results[0]["out_0_dram"]
```

```python
from contextlib import ExitStack

import numpy as np

import concourse.bass as bass
from concourse import mybir

F32 = mybir.dt.float32
F32R = mybir.dt.float32r
ALU = mybir.AluOpType
ACT = mybir.ActivationFunctionType
AX_X = mybir.AxisListType.X

B, N, C = 4, 256, 64
HALF = 128
HEADS = 4
HD = C // HEADS
PAIRS = HEADS // 2
GROUPS = 8
SCALE = float(C) ** -0.5
EPS0, EPS1 = 1e-5, 1e-3
HW = 32
RING = 4
PROJ = 2

_cols = {}
_width = [0]


def _place(*names_and_widths):
    for name, width in names_and_widths:
        _cols[name] = (_width[0], _width[0] + width)
        _width[0] += width
    return _width[0]


END_A = _place(("ident", 128), ("group", C), ("vec", 16))
END_B = _place(("qk", 4 * 128), ("v0", C), ("ksub", 128))
WIDTH = _place(("out0", C), ("eye2", C), ("q1", 128), ("k1", 128), ("v1t", 128), ("p1", C), ("bp", C))
V_SCALE0, V_BIAS0, V_SCALE1, V_BIAS1, V_BQ, V_BK, V_BV, V_QMASK = range(8)


def _tiles(text):
    return tuple((name, *map(int, numbers)) for name, *numbers in (word.split(".") for word in text.split()))


RING_TILES = _tiles("""
    X.0 X.1 X.2 X.3 S.0.0 S.0.1 S.0.2 T.0.0 S.0.3 T.0.1 S.1.0 T.0.2 S.1.1 T.0.3 S.1.2 S.1.3 S.2.0 T.1.0
    T.1.1 T.1.2 S.2.1 T.1.3 T.2.0 S.2.2 S.2.3 T.2.1 S.3.0 S.3.1 T.2.2 T.2.3 T.3.0 S.3.2 S.3.3 T.3.1
    T.3.2 T.3.3 S1.0 T1.0 S1.1 T1.1 S1.2 T1.2 S1.3 T1.3""")
PROJ_TILES = _tiles("""
    WV Q.0 K.0 K.1 Q.1 K.2 Q.2 V.0 Q.3 K.3 V.1 V.2 V.3 Q1.0 K1.0 VN.0 Q1.1 VN.1 K1.1 K1.2 Q1.2 VN.2 Q1.3
    K1.3 VN.3""")
O_TILES = _tiles("""
    PV.0 PV.1 PV.2 PV.3 PV1.0 PV1.1 PV1.2 PV1.3""")

def tokens(dram):
    return dram.rearrange("b h w c -> b (h w) c").rearrange("b (p t) c -> p b (t c)", t=2)


def build(nc, x, params, out):
    with ExitStack() as ctx:
        def sb(name, shape, dt=F32):
            return ctx.enter_context(nc.sbuf_tensor(name, shape, dt))

        def sem(name):
            return ctx.enter_context(nc.semaphore(name))

        par = sb("par", [128, WIDTH])

        def P(name):
            a, z = _cols[name]
            return par[:, a:z]

        def V(i, rows=C):
            a = _cols["vec"][0] + i
            return par[0:rows, a:a + 1]

        xin = sb("xin", [128, B, HALF])
        wqk_h, wqk_l = sb("wqk_h", [128, 4, 128], F32R), sb("wqk_l", [128, 4, 128], F32R)
        wv0_h, wv0_l = sb("wv0_h", [128, C], F32R), sb("wv0_l", [128, C], F32R)
        wq1_h, wq1_l = sb("wq1_h", [128, 128], F32R), sb("wq1_l", [128, 128], F32R)
        wk1_h, wk1_l = sb("wk1_h", [128, 128], F32R), sb("wk1_l", [128, 128], F32R)
        wvn_h = sb("wvn_h", [128, 2, C], F32R)
        wvp_l = sb("wvp_l", [128, C], F32R)
        ident = sb("ident", [128, 128], F32R)
        ksub = sb("ksub", [128, 128], F32R)
        eye_y = sb("eye_y", [128, 2, C], F32R)
        row = sb("row", [1, C])
        ones_row = sb("ones_row", [1, 128])
        half = sb("half", [C, B])
        bn = sb("bn", [C, 2, B, 6])
        mv = sb("mv", [C, 2, B, 2])
        dev = sb("dev", [C, 2, B])
        spread = sb("spread", [C, 2, B])
        nmean = sb("nmean", [C, 2, B])
        var = sb("var", [C, 2, B])
        rstd = sb("rstd", [C, 2, B])
        sc = sb("sc", [C, 2, B])
        tb = sb("tb", [C, 2, B])
        xn0 = sb("xn0", [C, B, N])
        xs0 = sb("xs0", [128, B, N], F32R)
        qs = sb("qs", [128, B, PAIRS, N], F32R)
        ks = sb("ks", [128, B, PAIRS, N], F32R)
        v0 = sb("v0", [128, B, 2, HEADS, HW])
        nmax = sb("nmax", [128, B, HEADS, 2], F32R)
        pt = sb("pt", [128, B, HEADS, 2, N])
        ot = sb("ot", [128, B, N])
        rden = sb("rden", [128, B, 8])
        rn = sb("rn", [128, B, 8, 32])
        rt = sb("rt", [128, B, N])
        xn1 = sb("xn1", [C, B, N])
        xs1 = sb("xs1", [128, B, N], F32R)
        qs1 = sb("qs1", [128, B, N], F32R)
        kh1, kl1 = sb("kh1", [128, B, N], F32R), sb("kl1", [128, B, N], F32R)
        vn = sb("vn", [128, B, 2, 2, C + 1])
        nmax1 = sb("nmax1", [128, B, 2], F32R)
        pt1 = sb("pt1", [128, B, 2, N])
        rden1 = sb("rden1", [128, B, 2])
        res = sb("res", [128, B, 2, C])

        ring = [ctx.enter_context(nc.psum_tensor(f"ring{i}", [128, 2, N], F32)) for i in range(RING)]
        proj = [ctx.enter_context(nc.psum_tensor(f"proj{i}", [128, 512], F32)) for i in range(PROJ)]
        bank_y = ctx.enter_context(nc.psum_tensor("bank_y", [128, 512], F32))
        bank_o = ctx.enter_context(nc.psum_tensor("bank_o", [128, 512], F32))
        HOP = N

        x_in = [sem(f"x_in{i}") for i in range(2)]
        a_in, b_in, c_in = sem("a_in"), sem("b_in"), sem("c_in")
        out_sent = sem("out_sent")
        const_ready = sem("const_ready")
        split_consts = sem("split_consts")
        w0_hi, w0_lo, w1_hi, w1_lo = sem("w0_hi"), sem("w0_lo"), sem("w1_hi"), sem("w1_lo")
        wvp_made, wvp_hi, wvp_ready = sem("wvp_made"), sem("wvp_hi"), sem("wvp_ready")
        xt_ready = sem("xt_ready")
        mean_ready, mean_hop = sem("mean_ready"), sem("mean_hop")
        spread_ready, spread_hop, nmean_ready = sem("spread_ready"), sem("spread_hop"), sem("nmean_ready")
        var_ready, rstd_ready = sem("var_ready"), sem("rstd_ready")
        tb_ready = sem("tb_ready")
        xn_ready, xhi_ready = sem("xn_ready"), sem("xhi_ready")
        xs_ready0, xs_ready = sem("xs_ready0"), sem("xs_ready")
        q_made, k_made, k_less, v_made = sem("q_made"), sem("k_made"), sem("k_less"), sem("v_made")
        q_hi, k_hi = sem("q_hi"), sem("k_hi")
        q_ready, k_ready, v_ready = sem("q_ready"), sem("k_ready"), sem("v_ready")
        s_made, s_max = sem("s_made"), sem("s_max")
        t_made, exp_done = sem("t_made"), sem("exp_done")
        pv_made, y_made = sem("pv_made"), sem("y_made")
        ot_ready, rden_ready, rn_ready, rt_ready = sem("ot_ready"), sem("rden_ready"), sem("rn_ready"), sem("rt_ready")
        xn1_ready, xhi1_ready, xs1_ready = sem("xn1_ready"), sem("xhi1_ready"), sem("xs1_ready")
        q1_made, k1_made, vn_made = sem("q1_made"), sem("k1_made"), sem("vn_made")
        q1_hi, k1_hi, vn_ready = sem("q1_hi"), sem("k1_hi"), sem("vn_ready")
        q1_ready, k1_ready = sem("q1_ready"), sem("k1_ready")
        s1_made, s1_max = sem("s1_made"), sem("s1_max")
        t1_made, exp1_done, pv1_made = sem("t1_made"), sem("exp1_done"), sem("pv1_made")
        res_ready = sem("res_ready")
        dve_step = sem("dve_step")

        read_by = {"X": xn_ready, "S": s_max, "T": exp_done, "S1": s1_max, "T1": exp1_done,
                   "WV": wvp_ready, "Q": q_ready, "K": k_ready, "V": v_ready, "Q1": q1_ready,
                   "K1": k1_ready, "VN": vn_ready, "PV": ot_ready, "PV1": res_ready}

        def bank(*tile):
            if tile in RING_TILES:
                return ring[RING_TILES.index(tile) % RING]
            return proj[PROJ_TILES.index(tile) % PROJ]

        def wait_bank(pe, tiles, *tile):
            before = tiles.index(tile) - {RING_TILES: RING, PROJ_TILES: PROJ, O_TILES: 1}[tiles]
            if before >= 0:
                name, image, head = (*tiles[before], 0, 0)[:3]
                pe.wait_ge(read_by[name], (HEADS * image + head if name in ("S", "T") else image) + 1)

        CHAINS = [(0, 0, 1), (0, 1, B)] + [(1, b, b + 1) for b in range(B)]

        def hop_tile(i):
            _, a, z = CHAINS[i]
            return (bank_o if i == 1 else bank_y)[0:C, HOP + a:HOP + z]

        block = ctx.enter_context(nc.Block())

        @block.sync
        def _(sp):
            sp.dma_start(xin[:, 0:1, :], tokens(x)[:, 0:1, :]).then_inc(x_in[0], 16)
            sp.dma_start(xin[:, 1:B, :], tokens(x)[:, 1:B, :]).then_inc(x_in[1], 16)
            sp.dma_start(par[:, END_B:WIDTH], params[:, END_B:WIDTH]).then_inc(c_in, 16)
            for b in range(B):
                sp.wait_ge(res_ready, b + 1)
                sp.dma_start(tokens(out)[:, b, :], res[:, b, :, :].rearrange("p t c -> p (t c)")).then_inc(out_sent, 16)
            sp.wait_ge(out_sent, 16 * B)

        @block.gpsimd
        def _(pool):
            nc.gpsimd.memset(half[:], -0.5).then_inc(const_ready, 1)
            nc.gpsimd.memset(ones_row[:], 1.0).then_inc(const_ready, 1)
            nc.gpsimd.memset(v0[:], 1.0).then_inc(const_ready, 1)
            nc.gpsimd.memset(rn[:, :, :, HD:HD + 1], 1.0).then_inc(const_ready, 1)
            nc.gpsimd.memset(rn[:, :, :, HD + 1:32], 0.0).then_inc(const_ready, 1)
            nc.gpsimd.memset(vn[:], 1.0).then_inc(const_ready, 1)

            def inverse_std(i):
                layer, a, z = CHAINS[i]
                pool.wait_ge(const_ready, 1)
                pool.wait_ge(var_ready, i + 1)
                nc.gpsimd.tensor_tensor(rstd[:, layer, a:z], var[:, layer, a:z], half[:, a:z],
                                        ALU.pow).then_inc(rstd_ready, 1)

            def x_lo(b):
                pool.wait_ge(xhi_ready, b + 1)
                nc.gpsimd.tensor_tensor(xs0[C:128, b, :], xn0[:, b, :], xs0[0:C, b, :].bitcast(F32),
                                        ALU.subtract).then_inc(xs_ready, 1)

            def weights1_lo():
                pool.wait_ge(w1_hi, 2)
                nc.gpsimd.tensor_tensor(wq1_l[:], P("q1"), wq1_h[:].bitcast(F32), ALU.subtract).then_inc(w1_lo, 1)
                nc.gpsimd.tensor_tensor(wk1_l[:], P("k1"), wk1_h[:].bitcast(F32), ALU.subtract).then_inc(w1_lo, 1)

            inverse_std(0)
            pool.wait_ge(rstd_ready, 1)
            inverse_std(1)
            pool.wait_ge(rstd_ready, 2)
            x_lo(1)
            pool.wait_ge(xs_ready, 1)
            x_lo(2)
            pool.wait_ge(xs_ready, 2)
            weights1_lo()
            pool.wait_ge(w1_lo, 2)
            x_lo(3)
            pool.wait_ge(xs_ready, 3)
            inverse_std(2)
            pool.wait_ge(rstd_ready, 3)
            inverse_std(3)
            pool.wait_ge(rstd_ready, 4)
            inverse_std(4)
            pool.wait_ge(rstd_ready, 5)
            inverse_std(5)

        @block.scalar
        def _(act):
            act.dma_start(par[:, 0:END_A], params[:, 0:END_A]).then_inc(a_in, 16)
            act.dma_start(par[:, END_A:END_B], params[:, END_A:END_B]).then_inc(b_in, 16)

            def weights0_hi():
                act.wait_ge(b_in, 16)
                nc.scalar.copy(wqk_h[:], P("qk").rearrange("p (m c) -> p m c", m=4)).then_inc(w0_hi, 1)
                nc.scalar.copy(wv0_h[:], P("v0")).then_inc(w0_hi, 1)

            def constants():
                act.wait_ge(a_in, 16)
                act.wait_ge(b_in, 16)
                nc.scalar.copy(ident[:], P("ident")).then_inc(split_consts, 1)
                nc.scalar.copy(ksub[:], P("ksub")).then_inc(split_consts, 1)

            def weights1_hi():
                act.wait_ge(c_in, 16)
                nc.scalar.copy(wq1_h[:], P("q1")).then_inc(w1_hi, 1)
                nc.scalar.copy(wk1_h[:], P("k1")).then_inc(w1_hi, 1)
                nc.scalar.copy(wvn_h[:, 1, :], P("eye2")).then_inc(w1_hi, 1)
                nc.scalar.copy(eye_y[:, 0, :], P("eye2")).then_inc(w1_hi, 1)
                nc.scalar.copy(eye_y[:, 1, :], P("eye2")).then_inc(w1_hi, 1)

            def weights_vp_hi():
                act.wait_ge(wvp_made, 1)
                nc.scalar.copy(wvn_h[:, 0, :], bank("WV")[:, 0:C]).then_inc(wvp_hi, 1)

            def x_norm(b):
                act.wait_ge(xt_ready, b + 1)
                act.wait_ge(tb_ready, 1 if b == 0 else 2)
                nc.scalar.activation(xn0[:, b, :], bank("X", b)[0:C, 0, :], ACT.Identity,
                                     bias=tb[:, 0, b:b + 1], scale=sc[:, 0, b:b + 1]).then_inc(xn_ready, 1)
                act.wait_ge(xn_ready, b + 1)
                nc.scalar.copy(xs0[0:C, b, :], xn0[:, b, :]).then_inc(xhi_ready, 1)

            def q_hi_part(b):
                act.wait_ge(q_made, b + 1)
                nc.scalar.copy(qs[:, b, :, :], bank("Q", b)[:, :].rearrange("p (m n) -> p m n", m=PAIRS)).then_inc(q_hi, 1)

            def k_hi_part(b):
                act.wait_ge(k_made, b + 1)
                nc.scalar.copy(ks[:, b, :, :], bank("K", b)[:, :].rearrange("p (m n) -> p m n", m=PAIRS)).then_inc(k_hi, 1)

            def k_all(b):
                act.wait_ge(k_less, b + 1)
                nc.scalar.copy(ks[:, b, :, :], bank("K", b)[:, :].rearrange("p (m n) -> p m n", m=PAIRS)).then_inc(k_ready, 1)

            def v_copy(b):
                act.wait_ge(const_ready, 3)
                act.wait_ge(v_made, b + 1)
                nc.scalar.copy(v0[:, b, :, :, 0:HD],
                               bank("V", b)[:, 0:2 * C].rearrange("p (t h d) -> p t h d", t=2, h=HEADS)).then_inc(v_ready, 1)

            def exp(b, h):
                act.wait_ge(t_made, HEADS * b + h + 1)
                nc.scalar.activation(pt[:, b, h, :, :], bank("T", b, h)[:, :, :], ACT.Exp,
                                     scale=SCALE).then_inc(exp_done, 1)

            def x_norm1(b):
                act.wait_ge(tb_ready, 3 + b)
                nc.scalar.activation(xn1[:, b, :], bank_y[0:C, 0:N], ACT.Identity,
                                     bias=tb[:, 1, b:b + 1], scale=sc[:, 1, b:b + 1]).then_inc(xn1_ready, 1)

            def x_hi1(b):
                act.wait_ge(xn1_ready, b + 1)
                nc.scalar.copy(xs1[0:C, b, :], xn1[:, b, :]).then_inc(xhi1_ready, 1)

            def q_hi1_part(b):
                act.wait_ge(q1_made, b + 1)
                nc.scalar.activation(qs1[0:C, b, :], bank("Q1", b)[0:C, 0:N], ACT.Identity, bias=V(V_BQ)).then_inc(q1_hi, 1)

            def k_hi1_part(b):
                act.wait_ge(k1_made, b + 1)
                nc.scalar.activation(kh1[:, b, :], bank("K1", b)[:, 0:N], ACT.Identity, bias=V(V_BK, 128)).then_inc(k1_hi, 1)

            def vn_copy(b):
                act.wait_ge(vn_made, b + 1)
                act.wait_ge(const_ready, 6)
                nc.scalar.copy(vn[:, b, :, :, 0:C],
                               bank("VN", b)[:, 0:N].rearrange("p (t g c) -> p t g c", t=2, g=2)).then_inc(vn_ready, 1)

            def exp1(b):
                act.wait_ge(t1_made, b + 1)
                nc.scalar.activation(pt1[:, b, :, :], bank("T1", b)[:, :, :], ACT.Exp, scale=SCALE).then_inc(exp1_done, 1)

            constants(); weights1_hi(); weights0_hi(); x_norm(0); weights_vp_hi(); x_norm(1); q_hi_part(0)
            k_hi_part(0); x_norm(2); k_all(0); k_hi_part(1); x_norm(3); k_all(1); q_hi_part(1); exp(0, 0)
            k_hi_part(2); exp(0, 1); q_hi_part(2); k_all(2); exp(0, 2); exp(0, 3); v_copy(0); q_hi_part(3)
            exp(1, 0); k_hi_part(3); exp(1, 1); exp(1, 2); v_copy(1); exp(1, 3); exp(2, 0); k_all(3)
            exp(2, 1); exp(2, 2); v_copy(2); x_norm1(0); exp(2, 3); x_hi1(0); exp(3, 0); v_copy(3)
            q_hi1_part(0); exp(3, 1); exp(3, 2); exp(3, 3); x_norm1(1); x_hi1(1); k_hi1_part(0); vn_copy(0)
            q_hi1_part(1); x_norm1(2); vn_copy(1); x_hi1(2); k_hi1_part(1); exp1(0); k_hi1_part(2)
            q_hi1_part(2); x_norm1(3); x_hi1(3); vn_copy(2); exp1(1); q_hi1_part(3); k_hi1_part(3); exp1(2)
            vn_copy(3); exp1(3)

        @block.vector
        def _(dve):
            steps = [0]

            def then(ins):
                ins.then_inc(dve_step, 1)
                steps[0] += 1
                dve.wait_ge(dve_step, steps[0])

            def channel_stats(i, tiles, made, counts):
                layer, a, z = CHAINS[i]
                for b in range(a, z):
                    dve.wait_ge(made, counts[b - a])
                    then(nc.vector.bn_stats(bn[:, layer, b, :], tiles[b - a]))
                    ins = nc.vector.bn_aggr(mv[:, layer, b, :], bn[:, layer, b, :])
                ins.then_inc(mean_ready, 1)
                dve.wait_ge(mean_ready, i + 1)

            def group_spread(i):
                layer, a, z = CHAINS[i]
                s = (slice(None), layer, slice(a, z))
                mean = mv[:, layer, a:z, 0]
                dve.wait_ge(mean_hop, i + 1)
                then(nc.vector.tensor_tensor(dev[s], mean, hop_tile(i), ALU.subtract))
                if z - a == 1:
                    nc.vector.scalar_tensor_tensor(spread[s], dev[s], dev[s], mv[:, layer, a:z, 1],
                                                   ALU.mult, ALU.add).then_inc(spread_ready, 1)
                else:
                    then(nc.vector.tensor_tensor(spread[s], dev[s], dev[s], ALU.mult))
                    nc.vector.tensor_tensor(spread[s], spread[s], mv[:, layer, a:z, 1], ALU.add).then_inc(spread_ready, 1)
                nc.vector.tensor_tensor(nmean[s], dev[s], mean, ALU.subtract).then_inc(nmean_ready, 1)

            def group_var(i):
                layer, a, z = CHAINS[i]
                dve.wait_ge(spread_hop, i + 1)
                nc.vector.tensor_scalar(var[:, layer, a:z], hop_tile(i), (EPS0, EPS1)[layer], None,
                                        ALU.add).then_inc(var_ready, 1)

            def scale_shift(i):
                layer, a, z = CHAINS[i]
                s = (slice(None), layer, slice(a, z))
                shift = V((V_BIAS0, V_BIAS1)[layer])
                dve.wait_ge(rstd_ready, i + 1)
                dve.wait_ge(nmean_ready, i + 1)
                then(nc.vector.tensor_scalar(sc[s], rstd[s], V((V_SCALE0, V_SCALE1)[layer]), None, ALU.mult))
                if z - a == 1:
                    nc.vector.scalar_tensor_tensor(tb[s], nmean[s], sc[s], shift, ALU.mult, ALU.add).then_inc(tb_ready, 1)
                else:
                    then(nc.vector.tensor_tensor(tb[s], nmean[s], sc[s], ALU.mult))
                    nc.vector.tensor_scalar(tb[s], tb[s], shift, None, ALU.add).then_inc(tb_ready, 1)

            def x_lo(b):
                dve.wait_ge(xhi_ready, 1)
                nc.vector.tensor_tensor(xs0[C:128, 0, :], xn0[:, 0, :], xs0[0:C, 0, :].bitcast(F32),
                                        ALU.subtract).then_inc(xs_ready0, 1)

            def weights0_lo():
                dve.wait_ge(w0_hi, 2)
                nc.vector.tensor_tensor(wqk_l[:], P("qk").rearrange("p (m c) -> p m c", m=4),
                                        wqk_h[:].bitcast(F32), ALU.subtract).then_inc(w0_lo, 1)
                nc.vector.tensor_tensor(wv0_l[:], P("v0"), wv0_h[:].bitcast(F32), ALU.subtract).then_inc(w0_lo, 1)

            def weights_vp_lo():
                dve.wait_ge(wvp_hi, 1)
                nc.vector.tensor_tensor(wvp_l[:], bank("WV")[:, 0:C], wvn_h[:, 0, :].bitcast(F32), ALU.subtract)
                nc.vector.tensor_tensor(row[:], bank("WV")[0:1, 128:128 + C], P("bp")[0:1, :], ALU.add).then_inc(wvp_ready, 1)

            def q_lo(b):
                dve.wait_ge(q_hi, b + 1)
                nc.vector.scalar_tensor_tensor(qs[:, b, :, :], qs[:, b, :, :].bitcast(F32), V(V_QMASK, 128),
                                               bank("Q", b)[:, :].rearrange("p (m n) -> p m n", m=PAIRS),
                                               ALU.mult, ALU.add).then_inc(q_ready, 1)

            def smax(b, h):
                dve.wait_ge(s_made, HEADS * b + h + 1)
                nc.vector.tensor_reduce(nmax[:, b, h, :], bank("S", b, h)[:, :, :], AX_X, ALU.max,
                                        negate=True).then_inc(s_max, 1)

            def out_turned(b):
                dve.wait_ge(pv_made, b + 1)
                nc.vector.transpose(ot[:, b, :], bank_o[:, 0:N]).then_inc(ot_ready, 1)

            def out_denominator(b):
                dve.wait_ge(ot_ready, b + 1)
                nc.vector.reciprocal(rden[:, b, :], blocks(b)[:, :, HD]).then_inc(rden_ready, 1)

            def out_divided(b):
                dve.wait_ge(rden_ready, b + 1)
                dve.wait_ge(const_ready, 5)
                nc.vector.tensor_tensor(rn[:, b, :, 0:HD], blocks(b)[:, :, 0:HD],
                                        rden[:, b, :].unsqueeze(2).broadcast_to([128, 8, HD]), ALU.mult).then_inc(rn_ready, 1)

            def out_turned_back(b):
                dve.wait_ge(rn_ready, b + 1)
                nc.vector.transpose(rt[:, b, :], rn[:, b, :, :].rearrange("p k r -> p (k r)")).then_inc(rt_ready, 1)

            def blocks(b):
                return ot[:, b, :].rearrange("p (k r) -> p k r", r=32)

            def x_lo1(b):
                dve.wait_ge(xhi1_ready, b + 1)
                nc.vector.tensor_tensor(xs1[C:128, b, :], xn1[:, b, :], xs1[0:C, b, :].bitcast(F32),
                                        ALU.subtract).then_inc(xs1_ready, 1)

            def q_lo1(b):
                dve.wait_ge(q1_hi, b + 1)
                nc.vector.scalar_tensor_tensor(qs1[C:128, b, :], bank("Q1", b)[0:C, 0:N], V(V_BQ),
                                               qs1[0:C, b, :].bitcast(F32), ALU.add, ALU.subtract).then_inc(q1_ready, 1)

            def k_lo1(b):
                dve.wait_ge(k1_hi, b + 1)
                nc.vector.scalar_tensor_tensor(kl1[:, b, :], bank("K1", b)[:, 0:N], V(V_BK, 128), kh1[:, b, :].bitcast(F32),
                                               ALU.add, ALU.subtract).then_inc(k1_ready, 1)

            def smax1(b):
                dve.wait_ge(s1_made, b + 1)
                nc.vector.tensor_reduce(nmax1[:, b, :], bank("S1", b)[:, :, :], AX_X, ALU.max,
                                        negate=True).then_inc(s1_max, 1)

            def final(b):
                dve.wait_ge(pv1_made, b + 1)
                o1 = bank_o[:, 0:2 * (C + 1)].rearrange("p (t c) -> p t c", t=2)
                then(nc.vector.reciprocal(rden1[:, b, :], o1[:, :, C]))
                for t in range(2):
                    ins = nc.vector.scalar_tensor_tensor(res[:, b, t, :], o1[:, t, 0:C], rden1[:, b, t:t + 1],
                                                         vn[:, b, t, 1, 0:C], ALU.mult, ALU.add)
                ins.then_inc(res_ready, 1)

            def stats(i):
                layer, a, z = CHAINS[i]
                if layer == 0:
                    channel_stats(i, [bank("X", b)[0:C, 0, :] for b in range(a, z)], xt_ready, [b + 1 for b in range(a, z)])
                else:
                    channel_stats(i, [bank_y[0:C, 0:N]], y_made, [a + 1])

            dve.wait_ge(a_in, 16)
            stats(0); stats(1); group_spread(0); group_spread(1); group_var(0); group_var(1); scale_shift(0)
            weights0_lo(); scale_shift(1); x_lo(0); weights_vp_lo(); q_lo(0); smax(0, 0); smax(0, 1); q_lo(1)
            smax(0, 2); smax(0, 3); smax(1, 0); q_lo(2); smax(1, 1); smax(1, 2); smax(1, 3); q_lo(3)
            out_turned(0); out_denominator(0); out_divided(0); out_turned_back(0); smax(2, 0); stats(2)
            smax(2, 1); smax(2, 2); smax(2, 3); group_spread(2); out_turned(1); smax(3, 0); out_denominator(1)
            group_var(2); smax(3, 1); scale_shift(2); out_divided(1); out_turned_back(1); smax(3, 2); x_lo1(0)
            stats(3); smax(3, 3); group_spread(3); out_turned(2); group_var(3); q_lo1(0); out_denominator(2)
            scale_shift(3); out_divided(2); out_turned_back(2); x_lo1(1); stats(4); k_lo1(0); group_spread(4)
            out_turned(3); group_var(4); out_denominator(3); out_divided(3); scale_shift(4); q_lo1(1)
            out_turned_back(3); smax1(0); x_lo1(2); stats(5); k_lo1(1); group_spread(5); k_lo1(2)
            group_var(5); smax1(1); scale_shift(5); final(0); q_lo1(2); x_lo1(3); smax1(2); q_lo1(3); k_lo1(3)
            final(1); smax1(3); final(2); final(3)

        @block.tensor
        def _(pe):
            def x_transpose(b):
                pe.wait_ge(x_in[min(b, 1)], 16)
                for t in range(2):
                    mm = pe.transpose(bank("X", b)[0:C, 0, t * HALF:(t + 1) * HALF], xin[:, b, C * t:C * (t + 1)],
                                      P("ident"))
                mm.then_inc(xt_ready, 1)

            def mean_hop_(i):
                layer, a, z = CHAINS[i]
                pe.wait_ge(mean_ready, i + 1)
                pe.matmul(hop_tile(i), P("group")[0:C, :], mv[:, layer, a:z, 0], start=True, stop=True).then_inc(mean_hop, 1)

            def spread_hop_(i):
                layer, a, z = CHAINS[i]
                pe.wait_ge(spread_ready, i + 1)
                pe.matmul(hop_tile(i), P("group")[0:C, :], spread[:, layer, a:z], start=True, stop=True).then_inc(spread_hop, 1)

            def weights_vp():
                pe.wait_ge(c_in, 16)
                wait_bank(pe, PROJ_TILES, "WV")
                pe.matmul(bank("WV")[:, 0:C], P("v1t")[0:C, :], P("p1")[0:C, :], start=True, stop=True)
                pe.matmul(bank("WV")[0:1, 128:128 + C], V(V_BV), P("p1")[0:C, :], start=True, stop=True).then_inc(wvp_made, 1)

            def x_split(b):
                if b == 0:
                    pe.wait_ge(xs_ready0, 1)
                else:
                    pe.wait_ge(xs_ready, b)

            def q_or_k(kind, b, first, made):
                pe.wait_ge(w0_lo, 1)
                x_split(b)
                wait_bank(pe, PROJ_TILES, kind, b)
                for p in range(PAIRS):
                    o = bank(kind, b)[:, p * N:(p + 1) * N]
                    pe.matmul(o, wqk_h[:, first + p, :], xs0[:, b, :], start=(p == 0), stop=False, skip_group_check=True)
                    mm = pe.matmul(o, wqk_l[:, first + p, :], xs0[:, b, :], start=False, stop=True, skip_group_check=True)
                mm.then_inc(made, 1)

            def q(b):
                q_or_k("Q", b, 0, q_made)

            def k(b):
                q_or_k("K", b, PAIRS, k_made)

            def k_minus_hi(b):
                pe.wait_ge(k_hi, b + 1)
                pe.wait_ge(split_consts, 2)
                pe.matmul(bank("K", b)[:, :], ksub[:, :], ks[:, b, :, :].rearrange("p m n -> p (m n)"),
                          start=False, stop=True, skip_group_check=True).then_inc(k_less, 1)

            def v(b):
                pe.wait_ge(w0_lo, 2)
                x_split(b)
                wait_bank(pe, PROJ_TILES, "V", b)
                for t in range(2):
                    o = bank("V", b)[:, t * C:(t + 1) * C]
                    x_t = xs0[:, b, t * HALF:(t + 1) * HALF]
                    pe.matmul(o, x_t, wv0_h[:, :], start=True, stop=False)
                    mm = pe.matmul(o, x_t, wv0_l[:, :], start=False, stop=True)
                mm.then_inc(v_made, 1)

            def rows(h):
                return slice(64 * (h % 2), 64 * (h % 2) + 64)

            def scores(b, h):
                pe.wait_ge(q_ready, b + 1)
                pe.wait_ge(k_ready, b + 1)
                wait_bank(pe, RING_TILES, "S", b, h)
                for t in range(2):
                    mm = pe.matmul(bank("S", b, h)[:, t, :], qs[rows(h), b, h // 2, t * HALF:(t + 1) * HALF],
                                   ks[rows(h), b, h // 2, :], start=True, stop=True)
                mm.then_inc(s_made, 1)

            def minus_max(o, nm):
                for t in range(2):
                    pe.matmul(o[:, :, t * HALF:(t + 1) * HALF], nm[:, t:t + 1].broadcast_to([128, 128]),
                              ident[:, :].unsqueeze(1).broadcast_to([128, 2, 128]),
                              start=(t == 0), stop=False, skip_group_check=True)

            def scores_t(b, h):
                pe.wait_ge(s_max, HEADS * b + h + 1)
                wait_bank(pe, RING_TILES, "T", b, h)
                pe.wait_ge(split_consts, 1)
                o = bank("T", b, h)
                minus_max(o, nmax[:, b, h, :])
                for t in range(2):
                    mm = pe.matmul(o[:, t, :], ks[rows(h), b, h // 2, t * HALF:(t + 1) * HALF],
                                   qs[rows(h), b, h // 2, :], start=False, stop=(t == 1), skip_group_check=True)
                mm.then_inc(t_made, 1)

            def pv(b):
                pe.wait_ge(v_ready, b + 1)
                pe.wait_ge(exp_done, HEADS * (b + 1))
                if b == 0:
                    pe.wait_ge(var_ready, 2)
                wait_bank(pe, O_TILES, "PV", b)
                for t in range(2):
                    for h in range(HEADS):
                        mm = pe.matmul(bank_o[HW * h:HW * (h + 1), 0:N], v0[:, b, t, h, :], pt[:, b, h, t, :],
                                       start=(t == 0), stop=(t == 1))
                mm.then_inc(pv_made, 1)

            def y_input(b):
                x_split(b)
                pe.wait_ge(w1_hi, 5)
                if b >= 1:
                    pe.wait_ge(xn1_ready, b)
                else:
                    pe.wait_ge(var_ready, 1)
                pe.matmul(bank_y[:, 0:N], eye_y[:, :, :].rearrange("p a c -> p (a c)"), xs0[:, b, :],
                          start=True, stop=False, skip_group_check=True)

            def y(b):
                pe.wait_ge(rt_ready, b + 1)
                pe.matmul(bank_y[0:C, 0:N], P("out0"), rt[:, b, :], start=False, stop=True,
                          skip_group_check=True).then_inc(y_made, 1)

            def q_or_k1(kind, b, hi, lo, made):
                pe.wait_ge(w1_lo, 2)
                pe.wait_ge(xs1_ready, b + 1)
                wait_bank(pe, PROJ_TILES, kind, b)
                o = bank(kind, b)[:, 0:N]
                pe.matmul(o, hi[:, :], xs1[:, b, :], start=True, stop=False)
                pe.matmul(o, lo[:, :], xs1[:, b, :], start=False, stop=True).then_inc(made, 1)

            def q1(b):
                q_or_k1("Q1", b, wq1_h, wq1_l, q1_made)

            def k1(b):
                q_or_k1("K1", b, wk1_h, wk1_l, k1_made)

            def vn1(b):
                pe.wait_ge(const_ready, 2)
                pe.wait_ge(wvp_ready, 1)
                pe.wait_ge(xs1_ready, b + 1)
                wait_bank(pe, PROJ_TILES, "VN", b)
                for t in range(2):
                    x_t = xs1[:, b, t * HALF:(t + 1) * HALF]
                    o = bank("VN", b)[:, t * 2 * C:(t + 1) * 2 * C]
                    pe.matmul(o, x_t, wvn_h[:, :, :].rearrange("p g c -> p (g c)"), start=True, stop=False)
                    pe.matmul(o[:, 0:C], x_t, wvp_l[:, :], start=False, stop=False)
                    mm = pe.matmul(o[:, C:2 * C], ones_row[0:1, :], row[0:1, :], start=False, stop=True)
                mm.then_inc(vn_made, 1)

            def scores1(b):
                pe.wait_ge(q1_ready, b + 1)
                pe.wait_ge(k1_ready, b + 1)
                wait_bank(pe, RING_TILES, "S1", b)
                for t in range(2):
                    o, q_t = bank("S1", b)[:, t, :], qs1[:, b, t * HALF:(t + 1) * HALF]
                    pe.matmul(o, q_t, kh1[:, b, :], start=True, stop=False)
                    mm = pe.matmul(o, q_t, kl1[:, b, :], start=False, stop=True)
                mm.then_inc(s1_made, 1)

            def scores1_t(b):
                pe.wait_ge(s1_max, b + 1)
                wait_bank(pe, RING_TILES, "T1", b)
                o = bank("T1", b)
                minus_max(o, nmax1[:, b, :])
                for t in range(2):
                    for part in (kh1, kl1):
                        mm = pe.matmul(o[:, t, :], part[:, b, t * HALF:(t + 1) * HALF], qs1[:, b, :],
                                       start=False, stop=(t == 1 and part is kl1), skip_group_check=True)
                mm.then_inc(t1_made, 1)

            def pv1(b):
                pe.wait_ge(vn_ready, b + 1)
                pe.wait_ge(exp1_done, b + 1)
                wait_bank(pe, O_TILES, "PV1", b)
                for t in range(2):
                    o = bank_o[:, t * (C + 1):(t + 1) * (C + 1)]
                    for j in range(2):
                        mm = pe.matmul(o, pt1[:, b, j, t * HALF:(t + 1) * HALF], vn[:, b, j, 0, :],
                                       start=(j == 0), stop=(j == 1))
                mm.then_inc(pv1_made, 1)

            pe.wait_ge(a_in, 16)
            x_transpose(0); x_transpose(1); x_transpose(2); x_transpose(3); weights_vp(); mean_hop_(0)
            mean_hop_(1); spread_hop_(0); spread_hop_(1); q(0); k(0); k_minus_hi(0); k(1); scores(0, 0)
            y_input(0); k_minus_hi(1); q(1); scores(0, 1); scores(0, 2); scores_t(0, 0); k(2); scores(0, 3)
            scores_t(0, 1); q(2); k_minus_hi(2); scores(1, 0); scores_t(0, 2); scores(1, 1); scores_t(0, 3)
            v(0); scores(1, 2); q(3); scores(1, 3); pv(0); scores(2, 0); k(3); scores_t(1, 0); v(1)
            scores_t(1, 1); scores_t(1, 2); y(0); scores(2, 1); scores_t(1, 3); scores_t(2, 0); scores(2, 2)
            mean_hop_(2); k_minus_hi(3); scores(2, 3); pv(1); scores_t(2, 1); scores(3, 0); v(2)
            spread_hop_(2); scores(3, 1); scores_t(2, 2); scores_t(2, 3); scores_t(3, 0); scores(3, 2); v(3)
            scores(3, 3); y_input(1); y(1); pv(2); q1(0); mean_hop_(3); scores_t(3, 1); scores_t(3, 2)
            spread_hop_(3); k1(0); scores_t(3, 3); y_input(2); y(2); pv(3); mean_hop_(4); vn1(0)
            spread_hop_(4); q1(1); scores1(0); vn1(1); k1(1); y_input(3); y(3); scores1_t(0); k1(2)
            mean_hop_(5); scores1(1); q1(2); spread_hop_(5); pv1(0); vn1(2); scores1_t(1); scores1(2); q1(3)
            k1(3); pv1(1); scores1_t(2); scores1(3); vn1(3); pv1(2); scores1_t(3); pv1(3)


def kernel(x, L0_conv_gn_scale, L0_conv_gn_bias, L0_conv_w_qkv, L0_conv_w_out, L0_conv_b_out,
           L1_conv_gamma, L1_conv_beta, L1_conv_Wq, L1_conv_bq, L1_conv_Wk, L1_conv_bk,
           L1_conv_Wv, L1_conv_bv, L1_conv_Wp, L1_conv_bp):
    import concourse.bacc as bacc
    from concourse.bass_utils import run_bass_kernel_spmd

    params = np.zeros((128, WIDTH), np.float32)

    def put(name, value, rows=slice(0, 128)):
        a, z = _cols[name]
        params[rows, a:z] = value

    def twice(w):
        return np.concatenate([w, w], axis=0)

    put("ident", np.eye(128))
    size = C // GROUPS
    put("group", np.kron(np.eye(GROUPS), np.full((size, size), 1.0 / size)), slice(0, C))
    for i, vec in ((V_SCALE0, L0_conv_gn_scale), (V_BIAS0, L0_conv_gn_bias),
                   (V_SCALE1, L1_conv_gamma), (V_BIAS1, L1_conv_beta), (V_BQ, L1_conv_bq),
                   (V_BK, L1_conv_bk), (V_BV, L1_conv_bv)):
        params[:, _cols["vec"][0] + i] = twice(np.asarray(vec))
    part = np.arange(128) % 64 // HD
    params[:, _cols["vec"][0] + V_QMASK] = np.where(part >= 2, -1.0, 0.0)
    put("ksub", np.diag(np.where(part % 2 == 1, -1.0, 0.0)))
    qkv = np.asarray(L0_conv_w_qkv).reshape(C, HEADS, 3, HD)
    stacks = [np.repeat(qkv[:, 2 * p:2 * p + 2, i, None, :], 4, axis=2).reshape(C, 128)
              for i in range(2) for p in range(PAIRS)]
    put("qk", twice(np.concatenate(stacks, axis=1)))
    put("v0", twice(qkv[:, :, 2, :].reshape(C, C)))
    w_out = np.zeros((HEADS, 32, C), np.float32)
    w_out[:, 0:HD, :] = np.asarray(L0_conv_w_out).reshape(HEADS, HD, C)
    w_out[0, HD, :] = np.asarray(L0_conv_b_out)
    put("out0", w_out.reshape(128, C))
    for name, w in (("q1", L1_conv_Wq), ("k1", L1_conv_Wk)):
        put(name, np.tile(np.asarray(w), (2, 2)))
    put("eye2", twice(np.eye(C)))
    put("v1t", np.tile(np.asarray(L1_conv_Wv).T, (2, 2)))
    put("p1", twice(np.asarray(L1_conv_Wp)))
    put("bp", np.asarray(L1_conv_bp)[None, :], slice(0, 1))

    arrays = {"x_dram": np.ascontiguousarray(x), "params_dram": params}
    nc = bacc.Bacc("TRN2", target_bir_lowering=False, num_devices=1)
    ins = [nc.dram_tensor(n, a.shape, mybir.dt.from_np(a.dtype), kind="ExternalInput").ap() for n, a in arrays.items()]
    out = nc.dram_tensor("out_0_dram", (B, 16, 16, C), F32, kind="ExternalOutput").ap()
    build(nc, ins[0], ins[1], out)
    return run_bass_kernel_spmd(nc, [arrays], core_ids=[0]).results[0]["out_0_dram"]
```

```python
from contextlib import ExitStack

import numpy as np

import concourse.bass as bass
from concourse import mybir

F32 = mybir.dt.float32
F32R = mybir.dt.float32r
ALU = mybir.AluOpType
ACT = mybir.ActivationFunctionType
AX_X = mybir.AxisListType.X

B, N, C = 4, 256, 64
HALF = 128
HEADS = 4
HD = C // HEADS
PAIRS = HEADS // 2
GROUPS = 8
SCALE = float(C) ** -0.5
EPS0, EPS1 = 1e-5, 1e-3
HW = 32
RING = 4
PROJ = 2
LO1_POOL = 3

_cols = {}
_width = [0]


def _place(*names_and_widths):
    for name, width in names_and_widths:
        _cols[name] = (_width[0], _width[0] + width)
        _width[0] += width
    return _width[0]


END_A = _place(("group", C), ("vec", 16))
END_B = _place(("qkv0", 3 * C), ("ksub", 128))
WIDTH = _place(("qk1", 2 * C), ("eye2", C), ("v1t", 2 * C), ("p1", C), ("bp", C), ("out0", C))
V_SCALE0, V_BIAS0, V_SCALE1, V_BIAS1, V_BQ, V_BK, V_BV, V_QMASK = range(8)


def _tiles(text):
    return tuple((name, *map(int, numbers)) for name, *numbers in (word.split(".") for word in text.split()))


RING_TILES = _tiles("""
    X.0 X.1 X.2 X.3 S.0.0 S.0.1 S.0.2 S.0.3 T.0.0 T.0.1 T.0.2 T.0.3 S.1.0 S.1.1 S.1.2 T.1.0 T.1.1 S.1.3
    T.1.2 S.2.0 T.1.3 S.2.1 S.2.2 T.2.0 S.2.3 T.2.1 T.2.2 S.3.0 T.2.3 S.3.1 S.3.2 T.3.0 T.3.1 S.3.3
    T.3.2 T.3.3 S1.0 S1.1 T1.0 T1.1 S1.2 PV1.0 PV1.1 T1.2 S1.3.0 S1.3.1 PV1.2 T1.3.0 T1.3.1 PV1.3.0
    PV1.3.1""")
PROJ_TILES = _tiles("""
    X2 WV K.0 Q.0 K.1 Q.1 V.0 Q.2 K.2 V.1 Q.3 K.3 V.2 V.3 Q1.0 K1.0 Q1.1 K1.1 VN.0 VN.1 Q1.2 K1.2 VN.2
    Q1.3 K1.3 VN.3""")


def tokens(dram):
    return dram.rearrange("b h w c -> b (h w) c").rearrange("b (p t) c -> p b (t c)", t=2)


def build(nc, x, params, out):
    with ExitStack() as ctx:
        def sb(name, shape, dt=F32):
            return ctx.enter_context(nc.sbuf_tensor(name, shape, dt))

        def sem(name):
            return ctx.enter_context(nc.semaphore(name))

        par = sb("par", [128, WIDTH])

        def P(name):
            a, z = _cols[name]
            return par[:, a:z]

        def V(i, rows=C):
            a = _cols["vec"][0] + i
            return par[0:rows, a:a + 1]

        def wide0(i):
            return P("qkv0")[:, i * C:(i + 1) * C].rearrange("p (m h d) -> p m h d", m=PAIRS, h=2).unsqueeze(3).broadcast_to(
                [128, PAIRS, 2, 4, HD])

        def wide1():
            return P("qk1").rearrange("p (i c) -> p i c", i=2).unsqueeze(2).broadcast_to([128, 2, 2, C])

        xin = sb("xin", [128, B, HALF])
        wqk_h, wqk_l = (sb(n, [128, 2, PAIRS, 2, 4, HD], F32R) for n in ("wqk_h", "wqk_l"))
        wv0_h, wv0_l = sb("wv0_h", [128, C], F32R), sb("wv0_l", [128, C], F32R)
        w1_h, w1_l = sb("w1_h", [128, 2, 2, C], F32R), sb("w1_l", [128, 2, 2, C], F32R)
        wvn_h = sb("wvn_h", [128, 3, C], F32R)
        wvp_l = sb("wvp_l", [128, C], F32R)
        ident = sb("ident", [128, 128], F32R)
        ksub = sb("ksub", [128, 128], F32R)
        row = sb("row", [C, C])
        row_s = sb("row_s", [C, C], F32R)
        share = sb("share", [C, 128])
        share_r = sb("share_r", [C, 128], F32R)
        idle = sb("idle", [128, 128], mybir.dt.bfloat16)
        eye = sb("eye", [128, 128])
        warm = sb("warm", [128, 1])
        half = sb("half", [C, B])
        bn = sb("bn", [C, 2, B, 6])
        mv = sb("mv", [C, 2, B, 2])
        dev = sb("dev", [C, 2, B])
        spread = sb("spread", [C, 2, B])
        nmean = sb("nmean", [C, 2, B])
        var = sb("var", [C, 2, B])
        rstd = sb("rstd", [C, 2, B])
        sc = sb("sc", [C, 2, B])
        tb = sb("tb", [C, 2, B])
        xn0 = sb("xn0", [C, B, N])
        xs0 = sb("xs0", [128, B, N], F32R)
        qs = sb("qs", [128, B, PAIRS, N], F32R)
        ks = sb("ks", [128, B, PAIRS, N], F32R)
        v0 = sb("v0", [128, B, 2, HEADS, HW])
        nmax = sb("nmax", [128, B, HEADS, 2], F32R)
        pt = sb("pt", [128, B, HEADS, 2, N])
        ot = sb("ot", [128, B, N])
        rden = sb("rden", [128, B, 8])
        rn = sb("rn", [128, B, 8, 32])
        rt = sb("rt", [128, B, N])
        xn1 = sb("xn1", [C, B, N])
        xs1 = sb("xs1", [128, B, N], F32R)
        qs1 = sb("qs1", [128, B, N], F32R)
        kh1, kl1 = sb("kh1", [128, B, N], F32R), sb("kl1", [128, B, N], F32R)
        vn = sb("vn", [128, B, 2, 2, C + 1])
        nmax1 = sb("nmax1", [128, B, 2], F32R)
        pt1 = sb("pt1", [128, B, 2, N])
        rden1 = sb("rden1", [128, B, 2])
        res = sb("res", [128, B, 2, C])

        ring = [ctx.enter_context(nc.psum_tensor(f"ring{i}", [128, 2, N], F32)) for i in range(RING)]
        proj = [ctx.enter_context(nc.psum_tensor(f"proj{i}", [128, 512], F32)) for i in range(PROJ)]
        bank_y = ctx.enter_context(nc.psum_tensor("bank_y", [128, 512], F32))
        bank_o = ctx.enter_context(nc.psum_tensor("bank_o", [128, 512], F32))
        HOP = N

        x_in = [sem(f"x_in{i}") for i in range(2)]
        a_in, b_in, c_in = sem("a_in"), sem("b_in"), sem("c_in")
        out_sent = sem("out_sent")
        const_ready = sem("const_ready")
        idle_ready, eye_zero, eye_ready = sem("idle_ready"), sem("eye_zero"), sem("eye_ready")
        split_consts = sem("split_consts")
        w0_hi, wq_lo, wk_lo, wv_lo = sem("w0_hi"), sem("wq_lo"), sem("wk_lo"), sem("wv_lo")
        w1_hi, w1_lo = sem("w1_hi"), sem("w1_lo")
        wvp_made, wvp_hi, wvp_ready = sem("wvp_made"), sem("wvp_hi"), sem("wvp_ready")
        xt_ready, x2_ready = sem("xt_ready"), sem("x2_ready")
        mean_ready, mean_hop = sem("mean_ready"), sem("mean_hop")
        spread_ready, spread_hop, nmean_ready = sem("spread_ready"), sem("spread_hop"), sem("nmean_ready")
        var_ready, rstd_ready = sem("var_ready"), sem("rstd_ready")
        sc_ready, tb_ready = sem("sc_ready"), sem("tb_ready")
        xn_ready, xhi_ready = sem("xn_ready"), sem("xhi_ready")
        xs_ready0, xs_ready = sem("xs_ready0"), sem("xs_ready")
        q_made, k_made, k_less, v_made = sem("q_made"), sem("k_made"), sem("k_less"), sem("v_made")
        q_hi, k_hi = sem("q_hi"), sem("k_hi")
        q_ready, k_ready, v_ready = sem("q_ready"), sem("k_ready"), sem("v_ready")
        s_made, s_max = sem("s_made"), sem("s_max")
        t_made, exp_done = sem("t_made"), sem("exp_done")
        pv_made, y_made = sem("pv_made"), sem("y_made")
        ot_ready, rden_ready, rn_ready, rt_ready = sem("ot_ready"), sem("rden_ready"), sem("rn_ready"), sem("rt_ready")
        xn1_ready, xhi1_ready, xs1_ready = sem("xn1_ready"), sem("xhi1_ready"), sem("xs1_ready")
        xs1_early = sem("xs1_early")
        q1_made, k1_made, vn_made = sem("q1_made"), sem("k1_made"), sem("vn_made")
        q1_hi, k1_hi, vn_ready = sem("q1_hi"), sem("k1_hi"), sem("vn_ready")
        q1_ready, k1_ready = sem("q1_ready"), sem("k1_ready")
        s1_made, s1_max = sem("s1_made"), sem("s1_max")
        t1_made, exp1_done, pv1_made = sem("t1_made"), sem("exp1_done"), sem("pv1_made")
        res_ready = sem("res_ready")
        dve_step = sem("dve_step")

        read_by = {"X": xn_ready, "X2": xhi_ready, "S": s_max, "T": exp_done, "S1": s1_max, "T1": exp1_done,
                   "WV": wvp_ready, "Q": q_ready, "K": k_ready, "V": v_ready, "Q1": q1_ready,
                   "K1": k1_ready, "VN": vn_ready, "PV1": res_ready}

        def bank(*tile):
            if tile in RING_TILES:
                return ring[RING_TILES.index(tile) % RING]
            return proj[PROJ_TILES.index(tile) % PROJ]

        def wait_bank(pe, tiles, *tile):
            before = tiles.index(tile) - (RING if tiles is RING_TILES else PROJ)
            if before >= 0:
                name, image, part = (*tiles[before], 0, 0)[:3]
                pe.wait_ge(read_by[name], (HEADS * image if name in ("S", "T") else image) + part + 1)

        def nth(b, half=0):
            return b + half + 1

        def token_tiles(t):
            return slice(t * HALF, (t + 1) * HALF)

        def o1_tile(b, *half):
            tiles = 2 - len(half)
            return bank("PV1", b, *half)[:, 0, 0:tiles * (C + 1)].rearrange("p (t c) -> p t c", t=tiles)

        CHAINS = [(0, 0, 1), (0, 1, B)] + [(1, b, b + 1) for b in range(B)]
        CHAINS0 = len(CHAINS) - B

        def chain_of(layer, b):
            return next(i for i, (l, a, z) in enumerate(CHAINS) if l == layer and a <= b < z)

        def stats_of(i):
            layer, _, z = CHAINS[i]
            return layer * B + z

        def hop_tile(i):
            _, a, z = CHAINS[i]
            return bank_y[0:C, HOP + a:HOP + z]

        block = ctx.enter_context(nc.Block())

        @block.sync
        def _(sp):
            sp.dma_start(xin[:, 0:1, :], tokens(x)[:, 0:1, :]).then_inc(x_in[0], 16)
            sp.dma_start(xin[:, 1:B, :], tokens(x)[:, 1:B, :]).then_inc(x_in[1], 16)
            sp.dma_start(par[:, END_B:WIDTH], params[:, END_B:WIDTH]).then_inc(c_in, 16)
            for b in range(B):
                sp.wait_ge(res_ready, nth(b, int(b == B - 1)))
                sp.dma_start(tokens(out)[:, b, :], res[:, b, :, :].rearrange("p t c -> p (t c)")).then_inc(out_sent, 16)
            sp.wait_ge(out_sent, 16 * B)

        @block.gpsimd
        def _(pool):
            nc.gpsimd.memset(idle[:], 1.0).then_inc(idle_ready, 1)
            nc.gpsimd.memset(eye[:], 0.0).then_inc(eye_zero, 1)
            pool.wait_ge(eye_zero, 1)
            nc.gpsimd.affine_select(out=eye[:, :], in_=eye[:, :], compare_op=ALU.not_equal, fill=1.0, base=0,
                                    pattern=[[-1, 128]], channel_multiplier=1).then_inc(eye_ready, 1)
            nc.gpsimd.memset(half[:], -0.5).then_inc(const_ready, 1)
            nc.gpsimd.memset(share[:], 1 / 32).then_inc(const_ready, 1)
            nc.gpsimd.memset(v0[:], 1.0).then_inc(const_ready, 1)
            nc.gpsimd.memset(rn[:, :, :, HD:HD + 1], 1.0).then_inc(const_ready, 1)
            nc.gpsimd.memset(rn[:, :, :, HD + 1:32], 0.0).then_inc(const_ready, 1)
            nc.gpsimd.memset(vn[:], 1.0).then_inc(const_ready, 1)

            def inverse_std(i):
                layer, a, z = CHAINS[i]
                pool.wait_ge(const_ready, 1)
                pool.wait_ge(var_ready, i + 1)
                nc.gpsimd.tensor_tensor(rstd[:, layer, a:z], var[:, layer, a:z], half[:, a:z],
                                        ALU.pow).then_inc(rstd_ready, 1)

            def x_lo(b):
                pool.wait_ge(xhi_ready, b + 1)
                nc.gpsimd.tensor_tensor(xs0[C:128, b, :], xn0[:, b, :], xs0[0:C, b, :].bitcast(F32),
                                        ALU.subtract).then_inc(xs_ready, 1)

            def x_lo1(b):
                pool.wait_ge(xhi1_ready, b + 1)
                nc.gpsimd.tensor_tensor(xs1[C:128, b, :], xn1[:, b, :], xs1[0:C, b, :].bitcast(F32),
                                        ALU.subtract).then_inc(xs1_early, 1)

            def weights_q_lo():
                pool.wait_ge(w0_hi, 2)
                nc.gpsimd.tensor_tensor(wqk_l[:, 0], wide0(0), wqk_h[:, 0].bitcast(F32), ALU.subtract).then_inc(wq_lo, 1)

            def weights1_lo():
                pool.wait_ge(w1_hi, 1)
                nc.gpsimd.tensor_tensor(w1_l[:], wide1(), w1_h[:].bitcast(F32), ALU.subtract).then_inc(w1_lo, 1)

            inverse_std(0)
            pool.wait_ge(rstd_ready, 1)
            weights_q_lo()
            pool.wait_ge(wq_lo, 1)
            inverse_std(1)
            pool.wait_ge(rstd_ready, 2)
            x_lo(1)
            pool.wait_ge(xs_ready, 1)
            x_lo(2)
            pool.wait_ge(xs_ready, 2)
            x_lo(3)
            pool.wait_ge(xs_ready, 3)
            weights1_lo()
            pool.wait_ge(w1_lo, 1)
            inverse_std(2)
            pool.wait_ge(rstd_ready, 3)
            x_lo1(0)
            pool.wait_ge(xs1_early, 1)
            inverse_std(3)
            pool.wait_ge(rstd_ready, 4)
            x_lo1(1)
            pool.wait_ge(xs1_early, 2)
            inverse_std(4)
            pool.wait_ge(rstd_ready, 5)
            x_lo1(2)
            pool.wait_ge(xs1_early, 3)
            inverse_std(5)

        @block.scalar
        def _(act):
            act.dma_start(par[:, 0:END_A], params[:, 0:END_A]).then_inc(a_in, 16)
            act.dma_start(par[:, END_A:END_B], params[:, END_A:END_B]).then_inc(b_in, 16)

            act.wait_ge(idle_ready, 1)
            nc.scalar.activation(warm[:], idle[:, 0:1], ACT.Exp)

            def weights0_hi():
                act.wait_ge(b_in, 16)
                nc.scalar.copy(wqk_h[:, 1], wide0(1)).then_inc(w0_hi, 1)
                nc.scalar.copy(wqk_h[:, 0], wide0(0)).then_inc(w0_hi, 1)
                nc.scalar.copy(wv0_h[:], P("qkv0")[:, 2 * C:3 * C]).then_inc(w0_hi, 1)

            def constants():
                act.wait_ge(eye_ready, 1)
                act.wait_ge(b_in, 16)
                nc.scalar.copy(ident[:], eye[:]).then_inc(split_consts, 1)
                nc.scalar.copy(ksub[:], P("ksub")).then_inc(split_consts, 1)
                act.wait_ge(const_ready, 2)
                nc.scalar.copy(share_r[:], share[:]).then_inc(split_consts, 1)

            def weights1_hi():
                act.wait_ge(c_in, 16)
                nc.scalar.copy(w1_h[:], wide1()).then_inc(w1_hi, 1)
                nc.scalar.copy(wvn_h[:, 1:3, :], P("eye2").unsqueeze(1).broadcast_to([128, 2, C])).then_inc(w1_hi, 1)

            def weights_vp_hi():
                act.wait_ge(wvp_made, 1)
                nc.scalar.copy(wvn_h[:, 0, :], bank("WV")[:, 0:C]).then_inc(wvp_hi, 1)

            def x_norm_hi():
                act.wait_ge(x2_ready, 1)
                act.wait_ge(sc_ready, 1)
                act.wait_ge(tb_ready, 1)
                nc.scalar.activation(xs0[0:C, 0, :], bank("X2")[0:C, 0:N], ACT.Identity,
                                     bias=tb[:, 0, 0:1], scale=sc[:, 0, 0:1]).then_inc(xhi_ready, 1)

            def x_norm(b):
                act.wait_ge(xt_ready, b + 1)
                act.wait_ge(sc_ready, chain_of(0, b) + 1)
                act.wait_ge(tb_ready, chain_of(0, b) + 1)
                nc.scalar.activation(xn0[:, b, :], bank("X", b)[0:C, 0, :], ACT.Identity,
                                     bias=tb[:, 0, b:b + 1], scale=sc[:, 0, b:b + 1]).then_inc(xn_ready, 1)

            def x_hi(b):
                act.wait_ge(xn_ready, b + 1)
                nc.scalar.copy(xs0[0:C, b, :], xn0[:, b, :]).then_inc(xhi_ready, 1)

            def q_hi_part(b):
                act.wait_ge(q_made, b + 1)
                nc.scalar.copy(qs[:, b, :, :], bank("Q", b)[:, :].rearrange("p (m n) -> p m n", m=PAIRS)).then_inc(q_hi, 1)

            def k_hi_part(b):
                act.wait_ge(k_made, b + 1)
                nc.scalar.copy(ks[:, b, :, :], bank("K", b)[:, :].rearrange("p (m n) -> p m n", m=PAIRS)).then_inc(k_hi, 1)

            def k_all(b):
                act.wait_ge(k_less, b + 1)
                nc.scalar.copy(ks[:, b, :, :], bank("K", b)[:, :].rearrange("p (m n) -> p m n", m=PAIRS)).then_inc(k_ready, 1)

            def v_copy(b):
                act.wait_ge(const_ready, 3)
                act.wait_ge(v_made, b + 1)
                nc.scalar.copy(v0[:, b, :, :, 0:HD],
                               bank("V", b)[:, 0:2 * C].rearrange("p (t h d) -> p t h d", t=2, h=HEADS)).then_inc(v_ready, 1)

            def exp(b, h):
                act.wait_ge(t_made, HEADS * b + h + 1)
                nc.scalar.activation(pt[:, b, h, :, :], bank("T", b, h)[:, :, :], ACT.Exp,
                                     scale=SCALE).then_inc(exp_done, 1)

            def x_norm1(b):
                act.wait_ge(sc_ready, chain_of(1, b) + 1)
                act.wait_ge(tb_ready, chain_of(1, b) + 1)
                nc.scalar.activation(xn1[:, b, :], bank_y[0:C, 0:N], ACT.Identity,
                                     bias=tb[:, 1, b:b + 1], scale=sc[:, 1, b:b + 1]).then_inc(xn1_ready, 1)

            def x_hi1(b):
                act.wait_ge(xn1_ready, b + 1)
                nc.scalar.copy(xs1[0:C, b, :], xn1[:, b, :]).then_inc(xhi1_ready, 1)

            def q_hi1_part(b):
                act.wait_ge(q1_made, b + 1)
                nc.scalar.activation(qs1[0:C, b, :], bank("Q1", b)[0:C, 0:N], ACT.Identity, bias=V(V_BQ)).then_inc(q1_hi, 1)

            def k_hi1_part(b):
                act.wait_ge(k1_made, b + 1)
                nc.scalar.activation(kh1[:, b, :], bank("K1", b)[:, 0:N], ACT.Identity, bias=V(V_BK, 128)).then_inc(k1_hi, 1)

            def vn_copy(b):
                act.wait_ge(vn_made, b + 1)
                act.wait_ge(const_ready, 6)
                nc.scalar.copy(vn[:, b, :, :, 0:C],
                               bank("VN", b)[:, 0:N].rearrange("p (t g c) -> p t g c", t=2, g=2)).then_inc(vn_ready, 1)

            def exp1(b, *half):
                act.wait_ge(t1_made, nth(b, *half))
                if half:
                    nc.scalar.activation(pt1[:, b, :, token_tiles(half[0])], bank("T1", b, *half)[:, 0, :].rearrange("p (t n) -> p t n", t=2),
                                         ACT.Exp, scale=SCALE).then_inc(exp1_done, 1)
                else:
                    nc.scalar.activation(pt1[:, b, :, :], bank("T1", b)[:, :, :], ACT.Exp, scale=SCALE).then_inc(exp1_done, 1)

            weights0_hi(); constants(); x_norm_hi(); weights_vp_hi(); weights1_hi(); k_hi_part(0); x_norm(1)
            q_hi_part(0); x_hi(1); k_all(0); x_norm(2); x_norm(3); k_hi_part(1); x_hi(2); q_hi_part(1)
            exp(0, 0); k_all(1); exp(0, 1); exp(0, 2); v_copy(0); exp(0, 3); q_hi_part(2); k_hi_part(2)
            x_hi(3); k_all(2); exp(1, 0); exp(1, 1); exp(1, 2); exp(1, 3); v_copy(1); q_hi_part(3); exp(2, 0)
            k_hi_part(3); x_norm1(0); k_all(3); exp(2, 1); exp(2, 2); x_hi1(0); exp(2, 3); v_copy(2)
            v_copy(3); exp(3, 0); x_norm1(1); q_hi1_part(0); x_hi1(1); k_hi1_part(0); exp(3, 1); exp(3, 2)
            exp(3, 3); q_hi1_part(1); k_hi1_part(1); x_norm1(2); vn_copy(0); x_hi1(2); vn_copy(1)
            k_hi1_part(2); q_hi1_part(2); exp1(0); exp1(1); x_norm1(3); x_hi1(3); vn_copy(2); q_hi1_part(3)
            k_hi1_part(3); exp1(2); vn_copy(3); exp1(3, 0); exp1(3, 1)

        @block.vector
        def _(dve):
            steps = [0]

            def then(ins):
                ins.then_inc(dve_step, 1)
                steps[0] += 1
                dve.wait_ge(dve_step, steps[0])

            def dve_then(ins):
                ins.then_inc(dve_step, 1)
                steps[0] += 1

            def dve_wait():
                dve.wait_ge(dve_step, steps[0])

            def channel_stats(layer, b, tile):
                then(nc.vector.bn_stats(bn[:, layer, b, :], tile))
                nc.vector.bn_aggr(mv[:, layer, b, :], bn[:, layer, b, :]).then_inc(mean_ready, 1)

            def stats(b):
                dve.wait_ge(xt_ready, b + 1)
                channel_stats(0, b, bank("X", b)[0:C, 0, :])

            def stats1(b):
                dve.wait_ge(y_made, b + 1)
                channel_stats(1, b, bank_y[0:C, 0:N])

            def group_spread(i):
                layer, a, z = CHAINS[i]
                s = (slice(None), layer, slice(a, z))
                dve.wait_ge(mean_hop, i + 1)
                dve.wait_ge(mean_ready, stats_of(i))
                dve_then(nc.vector.tensor_tensor(dev[s], mv[:, layer, a:z, 0], hop_tile(i), ALU.subtract))
                nc.vector.tensor_scalar(nmean[s], hop_tile(i), V((V_SCALE0, V_SCALE1)[layer]), -1.0,
                                        ALU.mult, ALU.mult).then_inc(nmean_ready, 1)
                dve_wait()
                if z - a == 1:
                    nc.vector.scalar_tensor_tensor(spread[s], dev[s], dev[s], mv[:, layer, a:z, 1],
                                                   ALU.mult, ALU.add).then_inc(spread_ready, 1)
                else:
                    then(nc.vector.tensor_tensor(spread[s], dev[s], dev[s], ALU.mult))
                    nc.vector.tensor_tensor(spread[s], spread[s], mv[:, layer, a:z, 1], ALU.add).then_inc(spread_ready, 1)

            def group_var(i):
                layer, a, z = CHAINS[i]
                dve.wait_ge(spread_hop, i + 1)
                nc.vector.tensor_scalar(var[:, layer, a:z], hop_tile(i), (EPS0, EPS1)[layer], None,
                                        ALU.add).then_inc(var_ready, 1)

            def scale_shift(i):
                layer, a, z = CHAINS[i]
                s = (slice(None), layer, slice(a, z))
                shift = V((V_BIAS0, V_BIAS1)[layer])
                dve.wait_ge(rstd_ready, i + 1)
                dve.wait_ge(nmean_ready, i + 1)
                if z - a > 1:
                    dve_then(nc.vector.tensor_tensor(tb[s], nmean[s], rstd[s], ALU.mult))
                nc.vector.tensor_scalar(sc[s], rstd[s], V((V_SCALE0, V_SCALE1)[layer]), None, ALU.mult).then_inc(sc_ready, 1)
                if z - a > 1:
                    dve_wait()
                    nc.vector.tensor_scalar(tb[s], tb[s], shift, None, ALU.add).then_inc(tb_ready, 1)
                else:
                    nc.vector.scalar_tensor_tensor(tb[s], nmean[s], rstd[s], shift, ALU.mult, ALU.add).then_inc(tb_ready, 1)

            def x_norm(b):
                dve.wait_ge(tb_ready, 1)
                nc.vector.tensor_scalar(xn0[:, 0, :], bank("X", 0)[0:C, 0, :], sc[:, 0, 0:1], tb[:, 0, 0:1],
                                        ALU.mult, ALU.add).then_inc(xn_ready, 1)

            def x_lo(b):
                dve.wait_ge(xn_ready, 1)
                dve.wait_ge(xhi_ready, 1)
                nc.vector.tensor_tensor(xs0[C:128, 0, :], xn0[:, 0, :], xs0[0:C, 0, :].bitcast(F32),
                                        ALU.subtract).then_inc(xs_ready0, 1)

            def weights0_lo():
                dve.wait_ge(w0_hi, 1)
                nc.vector.tensor_tensor(wqk_l[:, 1], wide0(1), wqk_h[:, 1].bitcast(F32), ALU.subtract).then_inc(wk_lo, 1)

            def weights_v_lo():
                dve.wait_ge(w0_hi, 3)
                nc.vector.tensor_tensor(wv0_l[:], P("qkv0")[:, 2 * C:3 * C], wv0_h[:].bitcast(F32), ALU.subtract).then_inc(wv_lo, 1)

            def weights_vp_lo():
                dve.wait_ge(wvp_hi, 1)
                nc.vector.tensor_tensor(wvp_l[:], bank("WV")[:, 0:C], wvn_h[:, 0, :].bitcast(F32), ALU.subtract)
                then(nc.vector.tensor_tensor(row[:], bank("WV")[0:C, 128:128 + C], P("bp")[0:C, :], ALU.add))
                then(nc.vector.tensor_copy(row_s[:], row[:]))
                nc.vector.scalar_tensor_tensor(row_s[:], row_s[:].bitcast(F32), V(V_QMASK), row[:],
                                               ALU.mult, ALU.add).then_inc(wvp_ready, 1)

            def q_lo(b):
                dve.wait_ge(q_hi, b + 1)
                nc.vector.scalar_tensor_tensor(qs[:, b, :, :], qs[:, b, :, :].bitcast(F32), V(V_QMASK, 128),
                                               bank("Q", b)[:, :].rearrange("p (m n) -> p m n", m=PAIRS),
                                               ALU.mult, ALU.add).then_inc(q_ready, 1)

            def smax(b, h):
                dve.wait_ge(s_made, HEADS * b + h + 1)
                nc.vector.tensor_reduce(nmax[:, b, h, :], bank("S", b, h)[:, :, :], AX_X, ALU.max,
                                        negate=True).then_inc(s_max, 1)

            def out_turned(b):
                dve.wait_ge(pv_made, b + 1)
                nc.vector.transpose(ot[:, b, :], bank_o[:, 0:N]).then_inc(ot_ready, 1)

            def out_denominator(b):
                dve.wait_ge(ot_ready, b + 1)
                nc.vector.reciprocal(rden[:, b, :], blocks(b)[:, :, HD]).then_inc(rden_ready, 1)

            def out_divided(b):
                dve.wait_ge(rden_ready, b + 1)
                dve.wait_ge(const_ready, 5)
                nc.vector.tensor_tensor(rn[:, b, :, 0:HD], blocks(b)[:, :, 0:HD],
                                        rden[:, b, :].unsqueeze(2).broadcast_to([128, 8, HD]), ALU.mult).then_inc(rn_ready, 1)

            def out_turned_back(b):
                dve.wait_ge(rn_ready, b + 1)
                nc.vector.transpose(rt[:, b, :], rn[:, b, :, :].rearrange("p k r -> p (k r)")).then_inc(rt_ready, 1)

            def blocks(b):
                return ot[:, b, :].rearrange("p (k r) -> p k r", r=32)

            def x_lo1(b):
                dve.wait_ge(xhi1_ready, b + 1)
                nc.vector.tensor_tensor(xs1[C:128, b, :], xn1[:, b, :], xs1[0:C, b, :].bitcast(F32),
                                        ALU.subtract).then_inc(xs1_ready, 1)

            def q_lo1(b):
                dve.wait_ge(q1_hi, b + 1)
                nc.vector.scalar_tensor_tensor(qs1[C:128, b, :], bank("Q1", b)[0:C, 0:N], V(V_BQ),
                                               qs1[0:C, b, :].bitcast(F32), ALU.add, ALU.subtract).then_inc(q1_ready, 1)

            def k_lo1(b):
                dve.wait_ge(k1_hi, b + 1)
                nc.vector.scalar_tensor_tensor(kl1[:, b, :], bank("K1", b)[:, 0:N], V(V_BK, 128), kh1[:, b, :].bitcast(F32),
                                               ALU.add, ALU.subtract).then_inc(k1_ready, 1)

            def smax1(b, *half):
                dve.wait_ge(s1_made, nth(b, *half))
                if half:
                    nc.vector.tensor_reduce(nmax1[:, b, half[0]:half[0] + 1], bank("S1", b, *half)[:, 0, :], AX_X, ALU.max,
                                            negate=True).then_inc(s1_max, 1)
                else:
                    nc.vector.tensor_reduce(nmax1[:, b, :], bank("S1", b)[:, :, :], AX_X, ALU.max,
                                            negate=True).then_inc(s1_max, 1)

            def final(b, *half):
                dve.wait_ge(pv1_made, nth(b, *half))
                o1 = o1_tile(b, *half)
                tiles = half or (0, 1)
                then(nc.vector.reciprocal(rden1[:, b, tiles[0]:tiles[-1] + 1], o1[:, :, C]))
                for i, t in enumerate(tiles):
                    ins = nc.vector.scalar_tensor_tensor(res[:, b, t, :], o1[:, i, 0:C], rden1[:, b, t:t + 1],
                                                         vn[:, b, t, 1, 0:C], ALU.mult, ALU.add)
                ins.then_inc(res_ready, 1)

            dve.wait_ge(a_in, 16)
            stats(0); stats(1); group_spread(0); stats(2); group_var(0); stats(3); weights0_lo()
            scale_shift(0); group_spread(1); x_norm(0); group_var(1); x_lo(0); weights_vp_lo(); scale_shift(1)
            q_lo(0); smax(0, 0); smax(0, 1); smax(0, 2); smax(0, 3); q_lo(1); weights_v_lo(); smax(1, 0)
            smax(1, 1); smax(1, 2); q_lo(2); out_turned(0); out_denominator(0); out_divided(0)
            out_turned_back(0); smax(1, 3); smax(2, 0); stats1(0); smax(2, 1); group_spread(2); smax(2, 2)
            group_var(2); q_lo(3); scale_shift(2); smax(2, 3); out_turned(1); out_denominator(1)
            out_divided(1); out_turned_back(1); smax(3, 0); stats1(1); smax(3, 1); group_spread(3); smax(3, 2)
            group_var(3); out_turned(2); out_denominator(2); scale_shift(3); out_divided(2)
            out_turned_back(2); smax(3, 3); q_lo1(0); stats1(2); k_lo1(0); group_spread(4); group_var(4)
            q_lo1(1); k_lo1(1); scale_shift(4); out_turned(3); out_denominator(3); out_divided(3)
            out_turned_back(3); smax1(0); stats1(3); smax1(1); group_spread(5); q_lo1(2); group_var(5)
            k_lo1(2); scale_shift(5); smax1(2); x_lo1(3); final(0); final(1); q_lo1(3); k_lo1(3); smax1(3, 0)
            smax1(3, 1); final(2); final(3, 0); final(3, 1)

        @block.tensor
        def _(pe):
            def x_transpose(b):
                pe.wait_ge(x_in[min(b, 1)], 16)
                for t in range(2):
                    mm = pe.transpose(bank("X", b)[0:C, 0, t * HALF:(t + 1) * HALF], xin[:, b, C * t:C * (t + 1)],
                                      eye[:, :])
                mm.then_inc(xt_ready, 1)

            def x_again():
                wait_bank(pe, PROJ_TILES, "X2")
                for t in range(2):
                    mm = pe.transpose(bank("X2")[0:C, t * HALF:(t + 1) * HALF], xin[:, 0, C * t:C * (t + 1)], eye[:, :])
                mm.then_inc(x2_ready, 1)

            def mean_hop_(i):
                layer, a, z = CHAINS[i]
                pe.wait_ge(a_in, 16)
                pe.wait_ge(mean_ready, stats_of(i))
                if i >= 1:
                    pe.wait_ge(var_ready, i)
                pe.matmul(hop_tile(i), P("group")[0:C, :], mv[:, layer, a:z, 0], start=True, stop=True).then_inc(mean_hop, 1)

            def spread_hop_(i):
                layer, a, z = CHAINS[i]
                pe.wait_ge(spread_ready, i + 1)
                pe.matmul(hop_tile(i), P("group")[0:C, :], spread[:, layer, a:z], start=True, stop=True).then_inc(spread_hop, 1)

            def weights_vp():
                pe.wait_ge(c_in, 16)
                wait_bank(pe, PROJ_TILES, "WV")
                pe.matmul(bank("WV")[:, 0:C], P("v1t")[0:C, :], P("p1")[0:C, :], start=True, stop=True)
                pe.matmul(bank("WV")[0:C, 128:128 + C], V(V_BV).broadcast_to([C, C]), P("p1")[0:C, :], start=True, stop=True).then_inc(wvp_made, 1)

            def x_split(b):
                if b == 0:
                    pe.wait_ge(xs_ready0, 1)
                else:
                    pe.wait_ge(xs_ready, b)

            def x_split1(b):
                if b < LO1_POOL:
                    pe.wait_ge(xs1_early, b + 1)
                else:
                    pe.wait_ge(xs1_ready, b - LO1_POOL + 1)

            def q_or_k(kind, b, i, low, made):
                pe.wait_ge(low, 1)
                x_split(b)
                wait_bank(pe, PROJ_TILES, kind, b)
                for p in range(PAIRS):
                    o = bank(kind, b)[:, p * N:(p + 1) * N]
                    pe.matmul(o, wqk_h[:, i, p].rearrange("p h r d -> p (h r d)"), xs0[:, b, :], start=(p == 0), stop=False, skip_group_check=True)
                    mm = pe.matmul(o, wqk_l[:, i, p].rearrange("p h r d -> p (h r d)"), xs0[:, b, :], start=False, stop=True, skip_group_check=True)
                mm.then_inc(made, 1)

            def q(b):
                q_or_k("Q", b, 0, wq_lo, q_made)

            def k(b):
                q_or_k("K", b, 1, wk_lo, k_made)

            def k_minus_hi(b):
                pe.wait_ge(k_hi, b + 1)
                pe.wait_ge(split_consts, 2)
                pe.matmul(bank("K", b)[:, :], ksub[:, :], ks[:, b, :, :].rearrange("p m n -> p (m n)"),
                          start=False, stop=True, skip_group_check=True).then_inc(k_less, 1)

            def v(b):
                pe.wait_ge(wv_lo, 1)
                x_split(b)
                wait_bank(pe, PROJ_TILES, "V", b)
                for t in range(2):
                    o = bank("V", b)[:, t * C:(t + 1) * C]
                    x_t = xs0[:, b, t * HALF:(t + 1) * HALF]
                    pe.matmul(o, x_t, wv0_h[:, :], start=True, stop=False)
                    mm = pe.matmul(o, x_t, wv0_l[:, :], start=False, stop=True)
                mm.then_inc(v_made, 1)

            def rows(h):
                return slice(64 * (h % 2), 64 * (h % 2) + 64)

            def scores(b, h):
                pe.wait_ge(q_ready, b + 1)
                pe.wait_ge(k_ready, b + 1)
                wait_bank(pe, RING_TILES, "S", b, h)
                for t in range(2):
                    mm = pe.matmul(bank("S", b, h)[:, t, :], qs[rows(h), b, h // 2, t * HALF:(t + 1) * HALF],
                                   ks[rows(h), b, h // 2, :], start=True, stop=True)
                mm.then_inc(s_made, 1)

            def minus_max(o, nm):
                for t in range(2):
                    pe.matmul(o[:, :, t * HALF:(t + 1) * HALF], nm[:, t:t + 1].broadcast_to([128, 128]),
                              ident[:, :].unsqueeze(1).broadcast_to([128, 2, 128]),
                              start=(t == 0), stop=False, skip_group_check=True)

            def scores_t(b, h):
                pe.wait_ge(s_max, HEADS * b + h + 1)
                wait_bank(pe, RING_TILES, "T", b, h)
                pe.wait_ge(split_consts, 1)
                o = bank("T", b, h)
                minus_max(o, nmax[:, b, h, :])
                for t in range(2):
                    mm = pe.matmul(o[:, t, :], ks[rows(h), b, h // 2, t * HALF:(t + 1) * HALF],
                                   qs[rows(h), b, h // 2, :], start=False, stop=(t == 1), skip_group_check=True)
                mm.then_inc(t_made, 1)

            def pv(b):
                pe.wait_ge(v_ready, b + 1)
                pe.wait_ge(exp_done, HEADS * (b + 1))
                if b >= 1:
                    pe.wait_ge(ot_ready, b)
                for t in range(2):
                    for h in range(HEADS):
                        mm = pe.matmul(bank_o[HW * h:HW * (h + 1), 0:N], v0[:, b, t, h, :], pt[:, b, h, t, :],
                                       start=(t == 0), stop=(t == 1))
                mm.then_inc(pv_made, 1)

            def y_input(b):
                x_split(b)
                pe.wait_ge(w1_hi, 2)
                if b >= 1:
                    pe.wait_ge(xn1_ready, b)
                else:
                    pe.wait_ge(var_ready, CHAINS0)
                pe.matmul(bank_y[:, 0:N], wvn_h[:, 1:3, :].rearrange("p g c -> p (g c)"), xs0[:, b, :],
                          start=True, stop=False, skip_group_check=True)

            def y(b):
                pe.wait_ge(rt_ready, b + 1)
                pe.matmul(bank_y[0:C, 0:N], P("out0"), rt[:, b, :], start=False, stop=True,
                          skip_group_check=True).then_inc(y_made, 1)

            def q_or_k1(kind, b, i, made):
                pe.wait_ge(w1_lo, 1)
                x_split1(b)
                wait_bank(pe, PROJ_TILES, kind, b)
                o = bank(kind, b)[:, 0:N]
                pe.matmul(o, w1_h[:, i].rearrange("p r c -> p (r c)"), xs1[:, b, :], start=True, stop=False)
                pe.matmul(o, w1_l[:, i].rearrange("p r c -> p (r c)"), xs1[:, b, :], start=False, stop=True).then_inc(made, 1)

            def q1(b):
                q_or_k1("Q1", b, 0, q1_made)

            def k1(b):
                q_or_k1("K1", b, 1, k1_made)

            def vn1(b):
                pe.wait_ge(split_consts, 3)
                pe.wait_ge(wvp_ready, 1)
                x_split1(b)
                wait_bank(pe, PROJ_TILES, "VN", b)
                for t in range(2):
                    x_t = xs1[:, b, t * HALF:(t + 1) * HALF]
                    o = bank("VN", b)[:, t * 2 * C:(t + 1) * 2 * C]
                    pe.matmul(o, x_t, wvn_h[:, 0:2, :].rearrange("p g c -> p (g c)"), start=(t == 0), stop=False,
                              skip_group_check=True)
                    pe.matmul(o[:, 0:C], x_t, wvp_l[:, :], start=False, stop=False, skip_group_check=True)
                mm = pe.matmul(bank("VN", b)[:, 0:N].rearrange("p (t g c) -> p t g c", t=2, g=2)[:, :, 1, :], share_r[:, :],
                               row_s[:, :].unsqueeze(1).broadcast_to([C, 2, C]), start=False, stop=True,
                               skip_group_check=True)
                mm.then_inc(vn_made, 1)

            def scores1(b, *half):
                pe.wait_ge(q1_ready, b + 1)
                pe.wait_ge(k1_ready, b + 1)
                wait_bank(pe, RING_TILES, "S1", b, *half)
                for i, t in enumerate(half or (0, 1)):
                    o, q_t = bank("S1", b, *half)[:, i, :], qs1[:, b, t * HALF:(t + 1) * HALF]
                    pe.matmul(o, q_t, kh1[:, b, :], start=True, stop=False)
                    mm = pe.matmul(o, q_t, kl1[:, b, :], start=False, stop=True)
                mm.then_inc(s1_made, 1)

            def scores1_t(b, *half):
                pe.wait_ge(s1_max, nth(b, *half))
                wait_bank(pe, RING_TILES, "T1", b, *half)
                o = bank("T1", b, *half)
                if half:
                    t = half[0]
                    o, queries = o[:, 0, :].rearrange("p (t n) -> p t n", t=2), token_tiles(t)
                    pe.matmul(o, nmax1[:, b, t:t + 1].broadcast_to([128, 128]),
                              ident[:, :].unsqueeze(1).broadcast_to([128, 2, 128]),
                              start=True, stop=False, skip_group_check=True)
                else:
                    minus_max(o, nmax1[:, b, :])
                    queries = slice(0, N)
                for j in range(2):
                    for part in (kh1, kl1):
                        mm = pe.matmul(o[:, j, :], part[:, b, token_tiles(j)], qs1[:, b, queries],
                                       start=False, stop=(j == 1 and part is kl1), skip_group_check=True)
                mm.then_inc(t1_made, 1)

            def pv1(b, *half):
                pe.wait_ge(vn_ready, b + 1)
                pe.wait_ge(exp1_done, nth(b, *half))
                wait_bank(pe, RING_TILES, "PV1", b, *half)
                o1 = o1_tile(b, *half)
                for i, t in enumerate(half or (0, 1)):
                    for j in range(2):
                        mm = pe.matmul(o1[:, i, :], pt1[:, b, j, token_tiles(t)], vn[:, b, j, 0, :],
                                       start=(j == 0), stop=(j == 1))
                mm.then_inc(pv1_made, 1)

            def keep_warm(times):
                for _ in range(times):
                    pe.matmul(bank_o[:, 0:128], idle[:, :], idle[:, :], start=True, stop=True)

            pe.wait_ge(idle_ready, 1)
            keep_warm(19)
            pe.wait_ge(eye_ready, 1)
            x_transpose(0); x_again(); x_transpose(1); x_transpose(2); mean_hop_(0); x_transpose(3)
            keep_warm(2); spread_hop_(0); keep_warm(9); mean_hop_(1); weights_vp(); keep_warm(3)
            spread_hop_(1); keep_warm(7); k(0); keep_warm(6); q(0); y_input(0); k_minus_hi(0); keep_warm(26)
            scores(0, 0); scores(0, 1); k(1); scores(0, 2); scores(0, 3); q(1); scores_t(0, 0); k_minus_hi(1)
            scores_t(0, 1); scores_t(0, 2); scores_t(0, 3); scores(1, 0); v(0); scores(1, 1); q(2)
            scores(1, 2); k(2); pv(0); k_minus_hi(2); scores_t(1, 0); scores_t(1, 1); scores(1, 3)
            scores_t(1, 2); scores(2, 0); y(0); scores_t(1, 3); scores(2, 1); scores(2, 2); v(1); mean_hop_(2)
            q(3); scores_t(2, 0); spread_hop_(2); scores(2, 3); k(3); pv(1); k_minus_hi(3); scores_t(2, 1)
            scores_t(2, 2); y_input(1); scores(3, 0); scores_t(2, 3); y(1); v(2); scores(3, 1); scores(3, 2)
            mean_hop_(3); pv(2); spread_hop_(3); v(3); scores_t(3, 0); scores_t(3, 1); scores(3, 3); q1(0)
            k1(0); y_input(2); y(2); scores_t(3, 2); scores_t(3, 3); mean_hop_(4); q1(1); k1(1)
            spread_hop_(4); pv(3); vn1(0); scores1(0); vn1(1); y_input(3); y(3); scores1(1); q1(2); k1(2)
            mean_hop_(5); scores1_t(0); spread_hop_(5); scores1_t(1); vn1(2); scores1(2); pv1(0); pv1(1)
            q1(3); k1(3); scores1_t(2); vn1(3); scores1(3, 0); scores1(3, 1); pv1(2); scores1_t(3, 0)
            scores1_t(3, 1); pv1(3, 0); pv1(3, 1)


def kernel(x, L0_conv_gn_scale, L0_conv_gn_bias, L0_conv_w_qkv, L0_conv_w_out, L0_conv_b_out,
           L1_conv_gamma, L1_conv_beta, L1_conv_Wq, L1_conv_bq, L1_conv_Wk, L1_conv_bk,
           L1_conv_Wv, L1_conv_bv, L1_conv_Wp, L1_conv_bp):
    import concourse.bacc as bacc
    from concourse.bass_utils import run_bass_kernel_spmd

    params = np.zeros((128, WIDTH), np.float32)

    def put(name, value, rows=slice(0, 128)):
        a, z = _cols[name]
        params[rows, a:z] = value

    def twice(w):
        return np.concatenate([w, w], axis=0)

    size = C // GROUPS
    put("group", np.kron(np.eye(GROUPS), np.full((size, size), 1.0 / size)), slice(0, C))
    for i, vec in ((V_SCALE0, L0_conv_gn_scale), (V_BIAS0, L0_conv_gn_bias),
                   (V_SCALE1, L1_conv_gamma), (V_BIAS1, L1_conv_beta), (V_BQ, L1_conv_bq),
                   (V_BK, L1_conv_bk), (V_BV, L1_conv_bv)):
        params[:, _cols["vec"][0] + i] = twice(np.asarray(vec))
    part = np.arange(128) % 64 // HD
    params[:, _cols["vec"][0] + V_QMASK] = np.where(part >= 2, -1.0, 0.0)
    put("ksub", np.diag(np.where(part % 2 == 1, -1.0, 0.0)))
    qkv = np.asarray(L0_conv_w_qkv).reshape(C, HEADS, 3, HD)
    put("qkv0", twice(qkv.transpose(0, 2, 1, 3).reshape(C, 3 * C)))
    w_out = np.zeros((HEADS, 32, C), np.float32)
    w_out[:, 0:HD, :] = np.asarray(L0_conv_w_out).reshape(HEADS, HD, C)
    w_out[0, HD, :] = np.asarray(L0_conv_b_out)
    put("out0", w_out.reshape(128, C))
    put("qk1", twice(np.concatenate([np.asarray(L1_conv_Wq), np.asarray(L1_conv_Wk)], axis=1)))
    put("eye2", twice(np.eye(C)))
    put("v1t", np.tile(np.asarray(L1_conv_Wv).T, (2, 2)))
    put("p1", twice(np.asarray(L1_conv_Wp)))
    put("bp", np.asarray(L1_conv_bp)[None, :])

    arrays = {"x_dram": np.ascontiguousarray(x), "params_dram": params}
    nc = bacc.Bacc("TRN2", target_bir_lowering=False, num_devices=1)
    ins = [nc.dram_tensor(n, a.shape, mybir.dt.from_np(a.dtype), kind="ExternalInput").ap() for n, a in arrays.items()]
    out = nc.dram_tensor("out_0_dram", (B, 16, 16, C), F32, kind="ExternalOutput").ap()
    build(nc, ins[0], ins[1], out)
    return run_bass_kernel_spmd(nc, [arrays], core_ids=[0]).results[0]["out_0_dram"]
```
